# Optimizing a Trainium2 kernel written in Bass

```python
import numpy as np
import jax
import jax.numpy as jnp

def _softmax(x, axis=-1):
    return jax.nn.softmax(x, axis=axis)

def _gelu(x):
    return jax.nn.gelu(x, approximate=True)

def _silu(x):
    return jax.nn.silu(x)

def _sigmoid(x):
    return jax.nn.sigmoid(x)

def _layernorm(x, axis=-1, eps=1e-05):
    m = jnp.mean(x, axis=axis, keepdims=True)
    v = jnp.var(x, axis=axis, keepdims=True)
    return (x - m) / jnp.sqrt(v + eps)

def _scatter_add(tgt, idx, src, axis=0):
    return tgt.at[idx].add(src)

def _segment_sum(src, seg, n):
    return jax.ops.segment_sum(src, seg, n)
kernel_name = 'mk_perceiver_d2_seqx_r2_08531b'

def setup_inputs(seed: int=0):
    np.random.seed(seed)
    _w = jnp.asarray

    def _rec_inputs():
        import jax
        import jax.numpy as jnp
        _rk = jax.random.key(seed)
        x = -0.0005146 + 1 * jax.random.normal(jax.random.fold_in(_rk, 1), (4, 128, 512), jnp.float32)
        _lenS = 128 - jax.random.randint(jax.random.fold_in(_rk, 7), (4,), 0, max(1, 128 // 4) + 1, jnp.int32)
        _lenS2 = 2048 - jax.random.randint(jax.random.fold_in(_rk, 8), (4,), 0, max(1, 2048 // 4) + 1, jnp.int32)
        _ctx_1024P = jax.random.normal(jax.random.fold_in(_rk, 11), (4, 16, 512), jnp.float32)
        _ctx_1024c = jax.random.dirichlet(jax.random.fold_in(_rk, 511), 0.3 * jnp.ones((16,), jnp.float32), (4, 2048))
        _ctx_1024t = jnp.einsum('bsk,bkd->bsd', _ctx_1024c, _ctx_1024P)
        _ctx_1024t = _ctx_1024t * jax.lax.rsqrt(jnp.mean(jnp.square(_ctx_1024t)) + 1e-12) * 0.953939
        ctx_1024 = -0.000392918 + 0.999932 * (_ctx_1024t + 0.3 * jax.random.normal(jax.random.fold_in(_rk, 611), (4, 2048, 512), jnp.float32))
        _validS = jnp.arange(128)[None, :] < _lenS[:, None]
        _validS2 = jnp.arange(2048)[None, :] < _lenS2[:, None]
        _causal = jnp.tril(jnp.ones((128, 128), dtype=bool))
        mask_BxS2_bf1 = jnp.ones((4, 2048), dtype=bool)
        mask_Bx1xS2_ik0 = jnp.where(jnp.broadcast_to(_validS2[:, None, :], (4, 1, 2048)), 0, 1).astype(jnp.int32)
        return (x, ctx_1024, mask_BxS2_bf1, mask_Bx1xS2_ik0)
    x, ctx_1024, mask_BxS2_bf1, mask_Bx1xS2_ik0 = _rec_inputs()

    def _L0_xattn_setup():
        import jax, jax.numpy as jnp
        import numpy as np
        DIM = 512
        DIM_LATENT = 512
        DIM_HEAD = 64
        HEADS = 16
        INNER = HEADS * DIM_HEAD

        def layernorm(x, g, b, eps=1e-05):
            m = jnp.mean(x, axis=-1, keepdims=True)
            v = jnp.mean((x - m) ** 2, axis=-1, keepdims=True)
            return (x - m) / jnp.sqrt(v + eps) * g + b

        def rmsnorm(x, gamma, eps=1e-08):
            n = jnp.linalg.norm(x, axis=-1, keepdims=True) * x.shape[-1] ** (-0.5)
            return x / jnp.maximum(n, eps) * gamma
        key = jax.random.key(seed)
        ks = jax.random.split(key, 8)
        b, n, m = (4, 2048, 256)
        x = jax.random.normal(ks[0], (b, n, DIM), dtype=jnp.float32)
        latents = jax.random.normal(ks[1], (b, m, DIM_LATENT), dtype=jnp.float32)
        mask = jnp.ones((b, n), dtype=bool)
        s = 0.02
        return {'x': x, 'latents': latents, 'mask': mask, 'ln_x_g': jnp.ones((DIM,), jnp.float32), 'ln_x_b': jnp.zeros((DIM,), jnp.float32), 'ln_l_g': jnp.ones((DIM_LATENT,), jnp.float32), 'ln_l_b': jnp.zeros((DIM_LATENT,), jnp.float32), 'qn_g': jnp.ones((DIM_HEAD,), jnp.float32), 'kn_g': jnp.ones((DIM_HEAD,), jnp.float32), 'Wq': jax.random.normal(ks[2], (DIM_LATENT, INNER), jnp.float32) * s, 'Wkv': jax.random.normal(ks[3], (DIM, 2 * INNER), jnp.float32) * s, 'Wout': jax.random.normal(ks[4], (INNER, DIM_LATENT), jnp.float32) * s, 'bout': jnp.zeros((DIM_LATENT,), jnp.float32)}
    _L0_xattn_all = _L0_xattn_setup()
    _L0_xattn_in = {k: v for k, v in _L0_xattn_all.items() if k in ('ln_x_g', 'ln_x_b', 'ln_l_g', 'ln_l_b', 'qn_g', 'kn_g', 'Wq', 'Wkv', 'Wout', 'bout')}
    del _L0_xattn_all

    def _L0_attn_setup():
        import jax, jax.numpy as jnp
        import numpy as np
        H, KV, D = (8, 2, 128)
        RD = D // 4
        ROPE_THETA = 10000.0

        def _rope_cos_sin(seq_len, dtype):
            inv_freq = 1.0 / ROPE_THETA ** (jnp.arange(0, RD, 2, dtype=jnp.float32) / RD)
            pos = jnp.arange(seq_len, dtype=jnp.float32)
            freqs = pos[:, None] * inv_freq[None, :]
            emb = jnp.concatenate([freqs, freqs], axis=-1)
            return (jnp.cos(emb).astype(dtype), jnp.sin(emb).astype(dtype))

        def _apply_partial_rope(x, cos, sin):
            x_rot, x_pass = (x[..., :RD], x[..., RD:])
            half = RD // 2
            rot = jnp.concatenate([-x_rot[..., half:], x_rot[..., :half]], axis=-1)
            x_rot = x_rot * cos[None, None] + rot * sin[None, None]
            return jnp.concatenate([x_rot, x_pass], axis=-1)
        key = jax.random.key(seed)
        ks = jax.random.split(key, 5)
        B, S, hid = (4, 1024, 512)
        s = 0.02
        return {'hidden_states': jax.random.normal(ks[0], (B, S, hid), jnp.float32), 'Wq': jax.random.normal(ks[1], (hid, H * D * 2), jnp.float32) * s, 'Wk': jax.random.normal(ks[2], (hid, KV * D), jnp.float32) * s, 'Wv': jax.random.normal(ks[3], (hid, KV * D), jnp.float32) * s, 'Wo': jax.random.normal(ks[4], (H * D, hid), jnp.float32) * s}
    _L0_attn_all = _L0_attn_setup()
    _L0_attn_in = {k: v for k, v in _L0_attn_all.items() if k in ('Wq', 'Wk', 'Wv', 'Wo')}
    del _L0_attn_all

    def _L0_ffn_setup():
        import jax, jax.numpy as jnp
        import numpy as np
        B, S, D, E, H = (2, 512, 512, 16, 1024)
        TOP_K = 2
        TEMP = 1.0
        key = jax.random.key(seed)
        ks = jax.random.split(key, 4)
        sc_d = 1.0 / np.sqrt(D)
        sc_h = 1.0 / np.sqrt(H)
        return {'x': jax.random.normal(ks[0], (B, S, D), dtype=jnp.float32), 'Wr': jax.random.normal(ks[1], (D, E), dtype=jnp.float32) * sc_d, 'br': jnp.zeros((E,), dtype=jnp.float32), 'W1': jax.random.normal(ks[2], (E, D, H), dtype=jnp.float32) * sc_d, 'b1': jnp.zeros((E, H), dtype=jnp.float32), 'W2': jax.random.normal(ks[3], (E, H, D), dtype=jnp.float32) * sc_h, 'b2': jnp.zeros((E, D), dtype=jnp.float32)}
    _L0_ffn_all = _L0_ffn_setup()
    _L0_ffn_in = {k: v for k, v in _L0_ffn_all.items() if k in ('Wr', 'br', 'W1', 'b1', 'W2', 'b2')}
    del _L0_ffn_all

    def _L1_xattn_setup():
        import jax, jax.numpy as jnp
        import numpy as np
        B, L, D, H = (4, 1024, 512, 16)
        DK = D // H
        key = jax.random.key(seed)
        ks = jax.random.split(key, 12)
        s = 1.0 / np.sqrt(D)
        inp = {'query': jax.random.normal(ks[0], (B, L, D), jnp.float32), 'key': jax.random.normal(ks[1], (B, L, D), jnp.float32), 'value': jax.random.normal(ks[2], (B, L, D), jnp.float32), 'mask': jax.random.randint(ks[3], (B, 1, L), 0, 2, jnp.int32), 'Wq': jax.random.normal(ks[4], (D, D), jnp.float32) * s, 'bq': jnp.zeros((D,), jnp.float32), 'Wk': jax.random.normal(ks[5], (D, D), jnp.float32) * s, 'bk': jnp.zeros((D,), jnp.float32), 'Wv': jax.random.normal(ks[6], (D, D), jnp.float32) * s, 'bv': jnp.zeros((D,), jnp.float32), 'Wo': jax.random.normal(ks[7], (D, D), jnp.float32) * s, 'bo': jnp.zeros((D,), jnp.float32)}
        return inp
    _L1_xattn_all = _L1_xattn_setup()
    _L1_xattn_in = {k: v for k, v in _L1_xattn_all.items() if k in ('Wq', 'bq', 'Wk', 'bk', 'Wv', 'bv', 'Wo', 'bo')}
    del _L1_xattn_all

    def _L1_attn_setup():
        import jax, jax.numpy as jnp
        import numpy as np
        B, S, D = (2, 2048, 512)
        LOOKBACK = 128
        TOPK = 16
        CHUNK = 32
        NEG = -1e+30

        def _phrase_states(h):
            b, seq, d = h.shape
            hc = h.reshape(b, seq // CHUNK, CHUNK, d)
            pref = jnp.cumsum(hc, axis=2)
            denom = jnp.arange(1, CHUNK + 1, dtype=h.dtype).reshape(1, 1, CHUNK, 1)
            return (pref / denom).reshape(b, seq, d)

        def _shift1(x):
            return jnp.pad(x, ((0, 0), (1, 0), (0, 0)))[:, :-1]
        key = jax.random.key(seed)
        ks = jax.random.split(key, 11)
        s = 0.02
        inp = {'h': jax.random.normal(ks[0], (B, S, D), jnp.float32)}
        names = ['q_w', 'k_w', 'v_w', 'pk_w', 'pv_w']
        for i, n in enumerate(names):
            inp[n] = jax.random.normal(ks[1 + i], (D, D), jnp.float32) * s
            inp[n.replace('_w', '_b')] = jax.random.normal(ks[6 + i], (D,), jnp.float32) * s
        return inp
    _L1_attn_all = _L1_attn_setup()
    _L1_attn_in = {k: v for k, v in _L1_attn_all.items() if k in ('q_w', 'q_b', 'k_w', 'k_b', 'v_w', 'v_b', 'pk_w', 'pk_b', 'pv_w', 'pv_b')}
    del _L1_attn_all

    def _L1_ffn_setup():
        import jax, jax.numpy as jnp
        import numpy as np
        QMAX = 127.0

        def _ste_round(v):
            return v + jax.lax.stop_gradient(jnp.round(v) - v)

        def _act_fake_quant(x, clip_factor):
            scale = jax.nn.sigmoid(clip_factor) * jnp.max(jnp.abs(x)) / QMAX
            return jnp.clip(_ste_round(x / scale), -QMAX - 1.0, QMAX) * scale

        def _weight_fake_quant(w):
            scale = jnp.max(jnp.abs(w), axis=1, keepdims=True) / QMAX
            return jnp.clip(_ste_round(w / scale), -QMAX - 1.0, QMAX) * scale
        key = jax.random.key(seed)
        k1, k2, k3, k4 = jax.random.split(key, 4)
        B, S, H, I = (8, 4096, 512, 1408)
        return {'x': jax.random.normal(k1, (B, S, H), dtype=jnp.float32), 'clip_x': jnp.full((1,), 4.0, dtype=jnp.float32), 'clip_down': jnp.full((1,), 4.0, dtype=jnp.float32), 'w_gate': jax.random.normal(k2, (I, H), dtype=jnp.float32) * 0.02, 'w_up': jax.random.normal(k3, (I, H), dtype=jnp.float32) * 0.02, 'w_down': jax.random.normal(k4, (H, I), dtype=jnp.float32) * 0.02}
    _L1_ffn_all = _L1_ffn_setup()
    _L1_ffn_in = {k: v for k, v in _L1_ffn_all.items() if k in ('clip_x', 'clip_down', 'w_gate', 'w_up', 'w_down')}
    del _L1_ffn_all
    return {'x': x, 'ctx_1024': ctx_1024, 'mask_BxS2_bf1': mask_BxS2_bf1, 'mask_Bx1xS2_ik0': mask_Bx1xS2_ik0, 'L0_xattn_ln_x_g': _L0_xattn_in['ln_x_g'], 'L0_xattn_ln_x_b': _L0_xattn_in['ln_x_b'], 'L0_xattn_ln_l_g': _L0_xattn_in['ln_l_g'], 'L0_xattn_ln_l_b': _L0_xattn_in['ln_l_b'], 'L0_xattn_qn_g': _L0_xattn_in['qn_g'], 'L0_xattn_kn_g': _L0_xattn_in['kn_g'], 'L0_xattn_Wq': _L0_xattn_in['Wq'], 'L0_xattn_Wkv': _L0_xattn_in['Wkv'], 'L0_xattn_Wout': _L0_xattn_in['Wout'], 'L0_xattn_bout': _L0_xattn_in['bout'], 'L0_attn_Wq': _L0_attn_in['Wq'], 'L0_attn_Wk': _L0_attn_in['Wk'], 'L0_attn_Wv': _L0_attn_in['Wv'], 'L0_attn_Wo': _L0_attn_in['Wo'], 'L0_ffn_Wr': _L0_ffn_in['Wr'], 'L0_ffn_br': _L0_ffn_in['br'], 'L0_ffn_W1': _L0_ffn_in['W1'], 'L0_ffn_b1': _L0_ffn_in['b1'], 'L0_ffn_W2': _L0_ffn_in['W2'], 'L0_ffn_b2': _L0_ffn_in['b2'], 'L1_xattn_Wq': _L1_xattn_in['Wq'], 'L1_xattn_bq': _L1_xattn_in['bq'], 'L1_xattn_Wk': _L1_xattn_in['Wk'], 'L1_xattn_bk': _L1_xattn_in['bk'], 'L1_xattn_Wv': _L1_xattn_in['Wv'], 'L1_xattn_bv': _L1_xattn_in['bv'], 'L1_xattn_Wo': _L1_xattn_in['Wo'], 'L1_xattn_bo': _L1_xattn_in['bo'], 'L1_attn_q_w': _L1_attn_in['q_w'], 'L1_attn_q_b': _L1_attn_in['q_b'], 'L1_attn_k_w': _L1_attn_in['k_w'], 'L1_attn_k_b': _L1_attn_in['k_b'], 'L1_attn_v_w': _L1_attn_in['v_w'], 'L1_attn_v_b': _L1_attn_in['v_b'], 'L1_attn_pk_w': _L1_attn_in['pk_w'], 'L1_attn_pk_b': _L1_attn_in['pk_b'], 'L1_attn_pv_w': _L1_attn_in['pv_w'], 'L1_attn_pv_b': _L1_attn_in['pv_b'], 'L1_ffn_clip_x': _L1_ffn_in['clip_x'], 'L1_ffn_clip_down': _L1_ffn_in['clip_down'], 'L1_ffn_w_gate': _L1_ffn_in['w_gate'], 'L1_ffn_w_up': _L1_ffn_in['w_up'], 'L1_ffn_w_down': _L1_ffn_in['w_down']}

def reference(x, ctx_1024, mask_BxS2_bf1, mask_Bx1xS2_ik0, L0_xattn_ln_x_g, L0_xattn_ln_x_b, L0_xattn_ln_l_g, L0_xattn_ln_l_b, L0_xattn_qn_g, L0_xattn_kn_g, L0_xattn_Wq, L0_xattn_Wkv, L0_xattn_Wout, L0_xattn_bout, L0_attn_Wq, L0_attn_Wk, L0_attn_Wv, L0_attn_Wo, L0_ffn_Wr, L0_ffn_br, L0_ffn_W1, L0_ffn_b1, L0_ffn_W2, L0_ffn_b2, L1_xattn_Wq, L1_xattn_bq, L1_xattn_Wk, L1_xattn_bk, L1_xattn_Wv, L1_xattn_bv, L1_xattn_Wo, L1_xattn_bo, L1_attn_q_w, L1_attn_q_b, L1_attn_k_w, L1_attn_k_b, L1_attn_v_w, L1_attn_v_b, L1_attn_pk_w, L1_attn_pk_b, L1_attn_pv_w, L1_attn_pv_b, L1_ffn_clip_x, L1_ffn_clip_down, L1_ffn_w_gate, L1_ffn_w_up, L1_ffn_w_down):
    import jax
    import jax.numpy as jnp

    def _L0_xattn_ref(x, latents, mask, ln_x_g, ln_x_b, ln_l_g, ln_l_b, qn_g, kn_g, Wq, Wkv, Wout, bout):
        import jax, jax.numpy as jnp
        import numpy as np
        DIM = 512
        DIM_LATENT = 512
        DIM_HEAD = 64
        HEADS = 16
        INNER = HEADS * DIM_HEAD

        def layernorm(x, g, b, eps=1e-05):
            m = jnp.mean(x, axis=-1, keepdims=True)
            v = jnp.mean((x - m) ** 2, axis=-1, keepdims=True)
            return (x - m) / jnp.sqrt(v + eps) * g + b

        def rmsnorm(x, gamma, eps=1e-08):
            n = jnp.linalg.norm(x, axis=-1, keepdims=True) * x.shape[-1] ** (-0.5)
            return x / jnp.maximum(n, eps) * gamma
        b, n, _ = x.shape
        m = latents.shape[1]
        h, d = (HEADS, DIM_HEAD)
        scale = d ** (-0.5)
        xn = layernorm(x, ln_x_g, ln_x_b)
        ln = layernorm(latents, ln_l_g, ln_l_b)
        q = (ln @ Wq).reshape(b, m, h, d).transpose(0, 2, 1, 3)
        kv = jnp.concatenate([xn @ Wkv, ln @ Wkv], axis=1)
        kv = kv.reshape(b, n + m, 2, h, d)
        k = kv[:, :, 0].transpose(0, 2, 1, 3)
        v = kv[:, :, 1].transpose(0, 2, 1, 3)
        qn = rmsnorm(q, qn_g) * scale
        kn = rmsnorm(k, kn_g)
        sim = jnp.einsum('bhid,bhjd->bhij', qn, kn)
        max_neg = -jnp.finfo(sim.dtype).max
        padded_mask = jnp.concatenate([mask, jnp.ones((b, m), bool)], axis=1)
        sim = jnp.where(padded_mask[:, None, None, :], sim, max_neg)
        attn = jax.nn.softmax(sim.astype(jnp.float32), axis=-1).astype(sim.dtype)
        out = jnp.einsum('bhij,bhjd->bhid', attn, v)
        out = out.transpose(0, 2, 1, 3).reshape(b, m, h * d)
        return out @ Wout + bout

    def _L0_attn_ref(hidden_states, Wq, Wk, Wv, Wo):
        import jax, jax.numpy as jnp
        import numpy as np
        H, KV, D = (8, 2, 128)
        RD = D // 4
        ROPE_THETA = 10000.0

        def _rope_cos_sin(seq_len, dtype):
            inv_freq = 1.0 / ROPE_THETA ** (jnp.arange(0, RD, 2, dtype=jnp.float32) / RD)
            pos = jnp.arange(seq_len, dtype=jnp.float32)
            freqs = pos[:, None] * inv_freq[None, :]
            emb = jnp.concatenate([freqs, freqs], axis=-1)
            return (jnp.cos(emb).astype(dtype), jnp.sin(emb).astype(dtype))

        def _apply_partial_rope(x, cos, sin):
            x_rot, x_pass = (x[..., :RD], x[..., RD:])
            half = RD // 2
            rot = jnp.concatenate([-x_rot[..., half:], x_rot[..., :half]], axis=-1)
            x_rot = x_rot * cos[None, None] + rot * sin[None, None]
            return jnp.concatenate([x_rot, x_pass], axis=-1)
        B, S, _ = hidden_states.shape
        G = H // KV
        qg = hidden_states @ Wq
        q, gate = (qg[..., :H * D], qg[..., H * D:])
        k = hidden_states @ Wk
        v = hidden_states @ Wv
        q = q.reshape(B, S, H, D).transpose(0, 2, 1, 3)
        k = k.reshape(B, S, KV, D).transpose(0, 2, 1, 3)
        v = v.reshape(B, S, KV, D).transpose(0, 2, 1, 3)
        cos, sin = _rope_cos_sin(S, q.dtype)
        q = _apply_partial_rope(q, cos, sin)
        k = _apply_partial_rope(k, cos, sin)
        qg4 = q.reshape(B, KV, G, S, D)
        scores = jnp.einsum('bkgsd,bktd->bkgst', qg4, k) / jnp.sqrt(jnp.asarray(D, q.dtype))
        attn = jax.nn.softmax(scores, axis=-1)
        out = jnp.einsum('bkgst,bktd->bkgsd', attn, v)
        out = out.reshape(B, H, S, D).transpose(0, 2, 1, 3).reshape(B, S, H * D)
        out = out * jax.nn.silu(gate)
        return out @ Wo

    def _L0_ffn_ref(x, Wr, br, W1, b1, W2, b2):
        import jax, jax.numpy as jnp
        import numpy as np
        B, S, D, E, H = (2, 512, 512, 16, 1024)
        TOP_K = 2
        TEMP = 1.0
        token_shape = x.shape[:-1]
        d = x.shape[-1]
        xt = x.reshape(-1, d)
        T = xt.shape[0]
        logits = (xt @ Wr + br) / TEMP
        probs = jax.nn.softmax(logits, axis=-1)
        w, idx = jax.lax.top_k(probs, TOP_K)
        w = w / jnp.clip(jnp.sum(w, axis=-1, keepdims=True), 1e-09)
        comb = jnp.zeros((T, E), dtype=xt.dtype)
        comb = comb.at[jnp.arange(T)[:, None], idx].add(w)
        h = jax.nn.gelu(jnp.einsum('td,edh->teh', xt, W1) + b1, approximate=False)
        o = jnp.einsum('teh,eho->teo', h, W2) + b2
        y = jnp.einsum('teo,te->to', o, comb)
        y = xt + y
        return y.reshape(*token_shape, d)

    def _L1_xattn_ref(query, key, value, mask, Wq, bq, Wk, bk, Wv, bv, Wo, bo):
        import jax, jax.numpy as jnp
        import numpy as np
        B, L, D, H = (4, 1024, 512, 16)
        DK = D // H
        nb = query.shape[0]

        def proj(x, W, b):
            return (x @ W.T + b).reshape(nb, -1, H, DK).transpose(0, 2, 1, 3)
        q = proj(query, Wq, bq)
        k = proj(key, Wk, bk)
        v = proj(value, Wv, bv)
        scale = 1.0 / jnp.sqrt(jnp.asarray(DK, q.dtype))
        score = jnp.einsum('bhqd,bhkd->bhqk', q, k) * scale
        m = mask[:, None, :, :]
        score = jnp.where(m == 0, jnp.asarray(-1000000000.0, score.dtype), score)
        p = jax.nn.softmax(score, axis=-1)
        x = jnp.einsum('bhqk,bhkd->bhqd', p, v)
        x = x.transpose(0, 2, 1, 3).reshape(nb, -1, H * DK)
        return x @ Wo.T + bo

    def _L1_attn_ref(h, q_w, q_b, k_w, k_b, v_w, v_b, pk_w, pk_b, pv_w, pv_b):
        import jax, jax.numpy as jnp
        import numpy as np
        B, S, D = (2, 2048, 512)
        LOOKBACK = 128
        TOPK = 16
        CHUNK = 32
        NEG = -1e+30

        def _phrase_states(h):
            b, seq, d = h.shape
            hc = h.reshape(b, seq // CHUNK, CHUNK, d)
            pref = jnp.cumsum(hc, axis=2)
            denom = jnp.arange(1, CHUNK + 1, dtype=h.dtype).reshape(1, 1, CHUNK, 1)
            return (pref / denom).reshape(b, seq, d)

        def _shift1(x):
            return jnp.pad(x, ((0, 0), (1, 0), (0, 0)))[:, :-1]
        b, seq, d = h.shape
        scale = 1.0 / np.sqrt(d)
        q = h @ q_w.T + q_b
        k = h @ k_w.T + k_b
        v = h @ v_w.T + v_b
        ph = _phrase_states(h)
        pk = ph @ pk_w.T + pk_b
        pv = ph @ pv_w.T + pv_b
        k_prev, v_prev = (_shift1(k), _shift1(v))
        pk_prev, pv_prev = (_shift1(pk), _shift1(pv))
        seq_score = jnp.einsum('bsd,bsd->bs', q, k_prev) * scale
        phr_score = jnp.einsum('bsd,bsd->bs', q, pk_prev) * scale
        k_pad = jnp.pad(k, ((0, 0), (LOOKBACK, 0), (0, 0)))
        t_idx = jnp.arange(seq)

        def step(_, l):
            kl = jax.lax.dynamic_slice_in_dim(k_pad, l, seq, axis=1)
            sc = jnp.einsum('bsd,bsd->bs', q, kl) * scale
            valid = t_idx + l >= LOOKBACK
            return (None, jnp.where(valid[None, :], sc, NEG))
        _, scores = jax.lax.scan(step, None, jnp.arange(LOOKBACK))
        scores = jnp.moveaxis(scores, 0, -1)
        top_sc, top_l = jax.lax.top_k(scores, TOPK)
        gidx = jnp.clip(t_idx[None, :, None] - LOOKBACK + top_l, 0, seq - 1)
        sem_v = jax.vmap(lambda vb, ib: vb[ib])(v, gidx)
        all_sc = jnp.concatenate([seq_score[..., None], top_sc, phr_score[..., None]], axis=-1)
        all_v = jnp.concatenate([v_prev[:, :, None, :], sem_v, pv_prev[:, :, None, :]], axis=2)
        w = jax.nn.softmax(all_sc, axis=-1)
        out = jnp.einsum('bsn,bsnd->bsd', w, all_v)
        return jnp.where(t_idx[None, :, None] > 0, out, jnp.zeros((), out.dtype))

    def _L1_ffn_ref(x, clip_x, clip_down, w_gate, w_up, w_down):
        import jax, jax.numpy as jnp
        import numpy as np
        QMAX = 127.0

        def _ste_round(v):
            return v + jax.lax.stop_gradient(jnp.round(v) - v)

        def _act_fake_quant(x, clip_factor):
            scale = jax.nn.sigmoid(clip_factor) * jnp.max(jnp.abs(x)) / QMAX
            return jnp.clip(_ste_round(x / scale), -QMAX - 1.0, QMAX) * scale

        def _weight_fake_quant(w):
            scale = jnp.max(jnp.abs(w), axis=1, keepdims=True) / QMAX
            return jnp.clip(_ste_round(w / scale), -QMAX - 1.0, QMAX) * scale
        xq = _act_fake_quant(x, clip_x[0])
        gate = jnp.einsum('bsh,ih->bsi', xq, _weight_fake_quant(w_gate))
        up = jnp.einsum('bsh,ih->bsi', xq, _weight_fake_quant(w_up))
        h = _act_fake_quant(jax.nn.silu(gate) * up, clip_down[0])
        return jnp.einsum('bsi,hi->bsh', h, _weight_fake_quant(w_down))
    x = x + _L0_xattn_ref(ctx_1024, _layernorm(x, axis=-1), mask_BxS2_bf1, L0_xattn_ln_x_g, L0_xattn_ln_x_b, L0_xattn_ln_l_g, L0_xattn_ln_l_b, L0_xattn_qn_g, L0_xattn_kn_g, L0_xattn_Wq, L0_xattn_Wkv, L0_xattn_Wout, L0_xattn_bout)
    x = x + _L0_attn_ref(_layernorm(x, axis=-1), L0_attn_Wq, L0_attn_Wk, L0_attn_Wv, L0_attn_Wo)
    x = x + _L0_ffn_ref(_layernorm(x, axis=-1), L0_ffn_Wr, L0_ffn_br, L0_ffn_W1, L0_ffn_b1, L0_ffn_W2, L0_ffn_b2)
    x = x + _L1_xattn_ref(_layernorm(x, axis=-1), ctx_1024, ctx_1024, mask_Bx1xS2_ik0, L1_xattn_Wq, L1_xattn_bq, L1_xattn_Wk, L1_xattn_bk, L1_xattn_Wv, L1_xattn_bv, L1_xattn_Wo, L1_xattn_bo)
    x = x + _L1_attn_ref(_layernorm(x, axis=-1), L1_attn_q_w, L1_attn_q_b, L1_attn_k_w, L1_attn_k_b, L1_attn_v_w, L1_attn_v_b, L1_attn_pk_w, L1_attn_pk_b, L1_attn_pv_w, L1_attn_pv_b)
    x = x + _L1_ffn_ref(_layernorm(x, axis=-1), L1_ffn_clip_x, L1_ffn_clip_down, L1_ffn_w_gate, L1_ffn_w_up, L1_ffn_w_down)
    return x

_drawn_inputs = setup_inputs


def setup_inputs(seed=0):
    import zlib

    import numpy as np

    out = dict(_drawn_inputs(seed))
    spreads = {'L0_xattn_ln_x_g': (1.0, 0.2),
     'L0_xattn_ln_x_b': (0.0, 0.1),
     'L0_xattn_ln_l_g': (1.0, 0.598),
     'L0_xattn_ln_l_b': (0.0, 0.353),
     'L0_xattn_qn_g': (1.0, 0.6),
     'L0_xattn_kn_g': (1.0, 0.6),
     'L0_xattn_bout': (0.0, 0.1),
     'L0_ffn_br': (0.0, 0.1),
     'L0_ffn_b1': (0.0, 0.321),
     'L0_ffn_b2': (0.0, 0.1),
     'L1_xattn_bq': (0.0, 0.701),
     'L1_xattn_bk': (0.0, 2.0),
     'L1_xattn_bv': (0.0, 0.1),
     'L1_xattn_bo': (0.0, 0.1)}
    factors = {'L0_attn_Wk': 6.098,
     'L1_attn_q_b': 8.0,
     'L1_attn_k_b': 64.0,
     'L1_attn_v_b': 6.232,
     'L1_attn_pk_w': 8.0,
     'L1_attn_pk_b': 64.0,
     'L1_attn_pv_w': 6.309,
     'L1_attn_pv_b': 54.853}
    for name, (base, spread) in spreads.items():
        noise = np.random.default_rng([zlib.crc32(name.encode()), seed]).standard_normal(out[name].shape)
        drawn = base * np.exp(spread * noise) if base else spread * noise
        out[name] = jnp.asarray(drawn.astype(out[name].dtype))
    for name, factor in factors.items():
        out[name] = (out[name] * factor).astype(out[name].dtype)
    return out
```

```python
from contextlib import ExitStack

import numpy as np

import concourse.bass as bass
from concourse import mybir

F32 = mybir.dt.float32
BF16 = mybir.dt.bfloat16
U8 = mybir.dt.uint8
I32 = mybir.dt.int32
ALU = mybir.AluOpType
ACT = mybir.ActivationFunctionType
AX = mybir.AxisListType

P = 128
B = 4
D = 512
C = D // P
TOK = B * P
S2 = 2048
NT = S2 // P
BIG = 1e30


class Steps:

    def __init__(self, eng, sem):
        self.eng, self.sem, self.base, self.n = eng, sem, 0, 0

    def __call__(self, ins):
        self.n += 1
        ins.then_inc(self.sem, 1)
        self.eng.wait_ge(self.sem, self.base + self.n)

    def at(self, base):
        self.base, self.n = base, 0


def heads(ap, d):
    return ap.rearrange("p (h d) -> p h d", d=d)


def per_head(ap, n, d):
    return ap.unsqueeze(2).to_broadcast([P, n, d])


def row(vec, n):
    return vec.rearrange("(a n) -> a n", a=1).broadcast_to([P, n])


class Norm:

    def __init__(self, sb, sem, tag):
        self.stats = sb(f"{tag}_stats", [P, B, 6], F32)
        self.mv = sb(f"{tag}_mv", [P, B, 2], F32)
        self.var = sb(f"{tag}_var", [P, B], F32)
        self.sd = sb(f"{tag}_sd", [P, B], F32)
        self.rstd = sb(f"{tag}_rstd", [P, B], F32)
        self.var_ready = sem(f"{tag}_var_ready")
        self.sd_ready = sem(f"{tag}_sd_ready")
        self.done = sem(f"{tag}_done")

    def vector(self, dve, step, dst, src, n=1):
        for b in range(B):
            last = dve.bn_stats(self.stats[:, b, :], src[:, b, :])
        step(last)
        for b in range(B):
            last = dve.bn_aggr(self.mv[:, b, :], self.stats[:, b, :])
        step(last)
        dve.tensor_scalar(self.var[:], self.mv[:, :, 1], 1e-5, None, ALU.add).then_inc(self.var_ready, 1)
        dve.wait_ge(self.sd_ready, n)
        step(dve.reciprocal(self.rstd[:], self.sd[:]))
        for b in range(B):
            dve.tensor_scalar(dst[:, b, :], src[:, b, :], self.mv[:, b, 0:1], self.rstd[:, b:b + 1],
                              ALU.subtract, ALU.mult).then_inc(self.done, 1)

    def scalar(self, act, n=1):
        act.wait_ge(self.var_ready, n)
        act.activation(self.sd[:], self.var[:], ACT.Sqrt).then_inc(self.sd_ready, 1)


H0, DH0 = 16, 64
INNER = H0 * DH0
QUADS = H0 // 4
PAIRS = H0 // 2
NT0 = NT + 1
S0 = NT0 * P


def cross0_prepare(nc, t, keep, sb, sem):
    ps = t["ps"]
    identf = t["identf"]
    w_hi, w_lo, q_hi, q_lo = keep["w_hi"], keep["w_lo"], keep["q_hi"], keep["q_lo"]
    X = sb("c0_x", [P, B, D], F32)
    L = sb("c0_l", [P, B, D], F32)
    LT = sb("c0_lt", [P, C, TOK], F32)
    lt_hi = sb("c0_lthi", [P, C, TOK], BF16)
    lt_lo = sb("c0_ltlo", [P, C, TOK], BF16)
    wq = sb("c0_wq", [P, C, INNER], F32)
    wst = sb("c0_wst", [P, 2, C, 512], F32)
    q32 = sb("c0_q32", [P, B, INNER], F32)
    sq = sb("c0_sq", [P, 2, 512], F32)
    ss = sb("c0_ss", [P, B, H0], F32)
    rn = sb("c0_rn", [P, B, H0], F32)
    gl = sb("c0_gl", [P, C], F32)
    bl = sb("c0_bl", [P, C], F32)
    gq = sb("c0_gq", [P, DH0], F32)
    gk = sb("c0_gk", [P, DH0], F32)
    gqk = sb("c0_gqk", [P, DH0], F32)
    n1, n2 = Norm(sb, sem, "c0n1"), Norm(sb, sem, "c0n2")
    x_in, vec_in, wq_in, id_in = sem("c0_x_in"), sem("c0_vec_in"), sem("c0_wq_in"), sem("c0_id_in")
    w_in = [sem("c0_w_in0"), sem("c0_w_in1")]
    w_hi_done, w_lo_done = sem("c0_w_hi"), sem("c0_w_lo")
    dve_step, act_step = sem("c0_dve"), sem("c0_act")
    l_tp, lt_done, lt_hi_done, lt_lo_done = sem("c0_l_tp"), sem("c0_lt"), sem("c0_lt_hi"), sem("c0_lt_lo")
    q_mm, q_sq, q_cp, q_ss = sem("c0_q_mm"), sem("c0_q_sq"), sem("c0_q_cp"), sem("c0_q_ss")
    ms_ready, sd_ready, qn_done = sem("c0_ms"), sem("c0_sd"), sem("c0_qn")
    q_tp, q_hi_done, q_lo_done = sem("c0_q_tp"), sem("c0_q_hi"), sem("c0_q_lo")
    lt_out = sem("c0_lt_out")
    QN = INNER // 512

    with nc.Block() as block:

        @block.sync
        def _(sp):
            sp.dma_start(X[:], t["x"].rearrange("b p d -> p b d")).then_inc(x_in, 16)
            sp.dma_start(identf[:], t["eye"]).then_inc(id_in, 16)
            for dst, src in ((gl, t["L0_xattn_ln_l_g_col"]), (bl, t["L0_xattn_ln_l_b_col"]),
                             (gq, row(t["L0_xattn_qn_g"], DH0)), (gk, row(t["L0_xattn_kn_g"], DH0))):
                sp.dma_start(dst[:], src).then_inc(vec_in, 16)
            sp.dma_start(wq[:], t["L0_xattn_Wq"].rearrange("(c p) n -> p c n", p=P)).then_inc(wq_in, 16)
            wkv = t["L0_xattn_Wkv"].rearrange("(c p) n -> p c n", p=P)
            for g in range(QUADS):
                if g >= 2:
                    sp.wait_ge(w_lo_done, g - 1)
                for half in range(2):
                    sp.dma_start(wst[:, g % 2, :, half * 256:half * 256 + 256],
                                 wkv[:, :, half * INNER + g * 256:half * INNER + g * 256 + 256])\
                      .then_inc(w_in[g % 2], 16)
            sp.wait_ge(lt_lo_done, C)
            sp.wait_ge(lt_hi_done, C)
            for b in range(B):
                sp.dma_start(t["lt_hi_d"][b], lt_hi[:, :, b * P:(b + 1) * P]).then_inc(lt_out, 16)
                sp.dma_start(t["lt_lo_d"][b], lt_lo[:, :, b * P:(b + 1) * P]).then_inc(lt_out, 16)
            sp.wait_ge(lt_out, 2 * B * 16)

        @block.gpsimd
        def _(pool):
            for g in range(QUADS):
                pool.wait_ge(w_hi_done, g + 1)
                pool.tensor_tensor(w_lo[:, :, g, :], wst[:, g % 2], w_hi[:, :, g, :],
                                   ALU.subtract).then_inc(w_lo_done, 1)

        @block.scalar
        def _(act):
            def split(g):
                act.wait_ge(w_in[g % 2], 32 * (g // 2 + 1))
                act.activation(w_hi[:, :, g, :], wst[:, g % 2], ACT.Copy).then_inc(w_hi_done, 1)

            n1.scalar(act)
            n2.scalar(act)
            act.wait_ge(vec_in, 64)
            for c in range(C):
                act.wait_ge(l_tp, c + 1)
                act.activation(LT[:, c, :], ps[:, c, :], ACT.Identity, bias=bl[:, c:c + 1],
                               scale=gl[:, c:c + 1]).then_inc(lt_done, 1)
            act.wait_ge(lt_done, C)
            for c in range(C):
                act.activation(lt_hi[:, c, :], LT[:, c, :], ACT.Copy).then_inc(lt_hi_done, 1)
            for g in range(2):
                split(g)
            for k in range(B * QN):
                act.wait_ge(q_mm, k + 1)
                if k >= 2:
                    act.wait_ge(q_ss, k - 1)
                act.activation(sq[:, k % 2, :], ps[:, 4 + k % 4, :], ACT.Square).then_inc(q_sq, 1)
                act.activation(q32[:, k // QN, (k % QN) * 512:(k % QN + 1) * 512], ps[:, 4 + k % 4, :],
                               ACT.Copy).then_inc(q_cp, 1)
            for g in range(2, QUADS):
                split(g)
            act.wait_ge(ms_ready, 1)
            act.activation(rn[:], ss[:], ACT.Sqrt).then_inc(sd_ready, 1)
            for p in range(PAIRS):
                act.wait_ge(q_tp, p + 1)
                act.activation(q_hi[:, p, :], ps[:, p % 4, :], ACT.Copy).then_inc(q_hi_done, 1)

        @block.vector
        def _(dve):
            step = Steps(dve, dve_step)
            dve.wait_ge(x_in, 16)
            n1.vector(dve, step, L, X)
            dve.wait_ge(n1.done, B)
            n2.vector(dve, step, L, L)
            dve.wait_ge(vec_in, 64)
            step(dve.tensor_tensor(gqk[:], gq[:], gk[:], ALU.mult))
            step(dve.tensor_scalar(gqk[:], gqk[:], DH0 ** -0.5, None, ALU.mult))
            for c in range(C):
                dve.wait_ge(lt_hi_done, c + 1)
                dve.tensor_tensor(lt_lo[:, c, :], LT[:, c, :], lt_hi[:, c, :], ALU.subtract)\
                   .then_inc(lt_lo_done, 1)
            for k in range(B * QN):
                dve.wait_ge(q_sq, k + 1)
                dve.tensor_reduce(ss[:, k // QN, (k % QN) * 8:(k % QN + 1) * 8], heads(sq[:, k % 2, :], DH0),
                                  AX.X, ALU.add).then_inc(q_ss, 1)
            dve.wait_ge(q_ss, B * QN)
            dve.tensor_scalar(ss[:], ss[:], 1.0 / DH0, 1e-16, ALU.mult, ALU.max).then_inc(ms_ready, 1)
            dve.wait_ge(sd_ready, 1)
            step(dve.reciprocal(rn[:], rn[:]))
            dve.wait_ge(q_cp, B * QN)
            for b in range(B):
                last = dve.tensor_tensor(heads(q32[:, b, :], DH0), heads(q32[:, b, :], DH0),
                                         per_head(rn[:, b, :], H0, DH0), ALU.mult)
            step(last)
            for b in range(B):
                dve.tensor_tensor(heads(q32[:, b, :], DH0), heads(q32[:, b, :], DH0),
                                  gqk[:].unsqueeze(1).to_broadcast([P, H0, DH0]), ALU.mult).then_inc(qn_done, 1)
            for p in range(PAIRS):
                dve.wait_ge(q_hi_done, p + 1)
                dve.tensor_tensor(q_lo[:, p, :], ps[:, p % 4, :], q_hi[:, p, :], ALU.subtract)\
                   .then_inc(q_lo_done, 1)

        @block.tensor
        def _(pe):
            pe.wait_ge(id_in, 16)
            pe.wait_ge(n2.done, B)
            for c in range(C):
                for b in range(B):
                    last = pe.transpose(ps[:, c, b * P:(b + 1) * P], L[:, b, c * P:(c + 1) * P], identf[:])
                last.then_inc(l_tp, 1)
            pe.wait_ge(lt_done, C)
            pe.wait_ge(wq_in, 16)
            for k in range(B * QN):
                b, n = k // QN, k % QN
                if k >= 4:
                    pe.wait_ge(q_cp, k - 3)
                for c in range(C):
                    last = pe.matmul(ps[:, 4 + k % 4, :], LT[:, c, b * P:(b + 1) * P],
                                     wq[:, c, n * 512:(n + 1) * 512], start=(c == 0), stop=(c == C - 1))
                last.then_inc(q_mm, 1)
            pe.wait_ge(qn_done, B)
            for p in range(PAIRS):
                if p >= 4:
                    pe.wait_ge(q_lo_done, p - 3)
                for b in range(B):
                    last = pe.transpose(ps[:, p % 4, b * P:(b + 1) * P], q32[:, b, p * P:(p + 1) * P], identf[:])
                last.then_inc(q_tp, 1)


def cross0_attend(nc, t, keep, sb, sem):
    ps = t["ps"]
    identf, identb, onesb = t["identf"], t["identb"], t["onesb"]
    w_hi, w_lo, q_hi, q_lo = keep["w_hi"], keep["w_lo"], keep["q_hi"], keep["q_lo"]
    xn = sb("a0_xn", [P, 4, D], F32)
    x_hi = sb("a0_xhi", [P, C, S0], BF16)
    x_lo = sb("a0_xlo", [P, C, S0], BF16)
    xf = sb("a0_xf", [P, 2, 512], F32)
    k_hi = sb("a0_khi", [P, 2, 2, S0], BF16)
    k_lo = sb("a0_klo", [P, 2, 2, S0], BF16)
    VW = 2 * DH0 + 1
    v = sb("a0_v", [P, 2, NT0, 4, VW], BF16)
    kraw = sb("a0_kraw", [P, 2, 4, 256], F32)
    sq = sb("a0_sq", [P, 4, 256], F32)
    ss = sb("a0_ss", [P, 16], F32)
    sdk = sb("a0_sdk", [P, 16], F32)
    rn = sb("a0_rn", [P, 16], F32)
    qb_hi = sb("a0_qbhi", [P, 2, 2, 256], BF16)
    qb_lo = sb("a0_qblo", [P, 2, 2, 256], BF16)
    p32 = sb("a0_p32", [P, 2, 512], F32)
    p_hi = sb("a0_phi", [P, 2, 512], BF16)
    p_lo = sb("a0_plo", [P, 2, 512], BF16)
    mrow8 = sb("a0_mrow8", [P, S2], U8)
    mrow = sb("a0_mrow", [P, S2], BF16)
    mcol8 = sb("a0_mcol8", [P, B, NT], U8)
    mcols = sb("a0_mcols", [P, B, NT], F32)
    mcol = sb("a0_mcol", [P, NT], F32)
    junk = sb("a0_junk", [P, 512], BF16)
    mx = sb("a0_mx", [P, 4, 5], F32)
    m4 = sb("a0_m4", [P, 4], F32)
    Dg = sb("a0_d", [P, 4, P], BF16)
    o32 = sb("a0_o32", [P, 4, DH0 + 1], F32)
    rs = sb("a0_rs", [P, 4], F32)
    ao = sb("a0_ao", [P, 2, 256], F32)
    gx = sb("a0_gx", [P, C], F32)
    bx = sb("a0_bx", [P, C], F32)
    st = sb("a0_st", [P, 4, 6], F32)
    mv = sb("a0_mv", [P, 4, 2], F32)
    va = sb("a0_va", [P, 4], F32)
    sd = sb("a0_sd", [P, 4], F32)
    rstd = sb("a0_rstd", [P, 4], F32)

    ctx_in, lat_in, vec_in, mrow_in = sem("a0_ctx_in"), sem("a0_lat_in"), sem("a0_vec_in"), sem("a0_mrow_in")
    var_ready, sd_ready, xn_ready = sem("a0_var"), sem("a0_sdr"), sem("a0_xn_ready")
    ln_tp, ln_evac, xhi_done, xlo_done = sem("a0_ln_tp"), sem("a0_ln_evac"), sem("a0_xhi_d"), sem("a0_xlo_d")
    proj_mm, vhi_done, vlo_done = sem("a0_proj"), sem("a0_vhi"), sem("a0_vlo")
    ss_done, ms_ready, ksd_ready, kn_ready = sem("a0_ss_d"), sem("a0_ms"), sem("a0_ksd"), sem("a0_kn")
    kt_tp, kthi_done, ktlo_done = sem("a0_kt_tp"), sem("a0_kthi"), sem("a0_ktlo")
    qb_ready, mrow_ready, mcol_ready, ones_ready = sem("a0_qb"), sem("a0_mrow_r"), sem("a0_mcol_r"), sem("a0_ones")
    max_mm, max_done, d_ready = sem("a0_max_mm"), sem("a0_max_done"), sem("a0_d_r")
    s_mm, exp_done, phi_done, plo_done, pv_mm = sem("a0_s"), sem("a0_exp"), sem("a0_phi_d"), sem("a0_plo_d"), sem("a0_pv")
    o_evac, ao_ready, ao_out = sem("a0_o"), sem("a0_ao_r"), [sem("a0_ao_out0"), sem("a0_ao_out1")]
    dve_step, zero_done, mcols_done = sem("a0_dve"), sem("a0_zero"), sem("a0_mcols_d")

    G0 = 5
    size = [4, 4, 4, 4, 1]
    after = {s: [] for s in range(NT0)}
    for j in range(4):
        after[4 * j + 3].append(("sum", j, 0))
        after[min(4 * j + 4, NT0 - 1)].append(("norm", j, 0))
        after[min(4 * j + 5, NT0 - 1)].append(("turn", j, 0))
        after[min(4 * j + 6, NT0 - 1)].append(("turn", j, 1))
    after[NT0 - 1] += [("sum", 4, 0), ("norm", 4, 0), ("turn", 4, 0), ("turn", 4, 1)]

    def bank_s(n):
        return n % 2

    PV = 2

    def bank_p(gg, s):
        return 3 + (NT0 * gg + s) % 2

    KT = 5

    def bank_m(g, k):
        return 6 + (NT0 * g + k) % 2

    def schedule(eng, first, unit):
        first()
        for g in range(QUADS):
            unit(0, g, False)
        for b in range(1, B):
            for g in range(QUADS):
                unit(b, g, (b, g) == (B - 1, QUADS - 1))

    with nc.Block() as block:

        @block.sync
        def _(sp):
            sp.dma_start(gx[:], t["L0_xattn_ln_x_g_col"]).then_inc(vec_in, 16)
            sp.dma_start(bx[:], t["L0_xattn_ln_x_b_col"]).then_inc(vec_in, 16)
            sp.dma_start(mcol8[:], t["mask0_col"]).then_inc(vec_in, 16)

            def load(bb, first):
                for j in range(4):
                    if not (first and j == 0):
                        sp.wait_ge(ln_tp, 16 * bb + 4 * j)
                    sp.dma_start(xn[:], t["ctx"][bb, j * 512:(j + 1) * 512, :].rearrange("(i p) d -> p i d", p=P))\
                      .then_inc(ctx_in, 16)
                    if j == 0:
                        if not first:
                            sp.wait_ge(proj_mm, 4 * NT0 * bb)
                        sp.dma_start(x_hi[:, :, S2:S0], t["lt_hi_d"][bb]).then_inc(lat_in, 16)
                        sp.dma_start(x_lo[:, :, S2:S0], t["lt_lo_d"][bb]).then_inc(lat_in, 16)

            def mask_row(bb, first):
                if not first:
                    sp.wait_ge(mrow_ready, bb)
                sp.dma_start(mrow8[:], t["mask0"][bass.ds(bb, 1), :].broadcast_to([P, S2])).then_inc(mrow_in, 16)

            def unit(b, g, last):
                if g == 3 and not last:
                    load(b + 1, False)
                    mask_row(b + 1, False)
                u = 4 * b + g
                sp.wait_ge(ao_ready, u + 1)
                sp.dma_start(t["ao_d"][b, :, g * 256:(g + 1) * 256], ao[:, g % 2, :]).then_inc(ao_out[g % 2], 16)

            def first():
                load(0, True)
                mask_row(0, True)

            schedule(sp, first, unit)
            for done in ao_out:
                sp.wait_ge(done, 16 * 2 * B)

        @block.gpsimd
        def _(pool):
            pool.memset(qb_hi[:], 0.0).then_inc(zero_done, 1)
            pool.memset(qb_lo[:], 0.0).then_inc(zero_done, 1)
            for par in range(2):
                pool.memset(v[:, par, :, :, DH0:DH0 + 1], 1.0).then_inc(ones_ready, 1)
            pool.wait_ge(zero_done, 2)
            pool.wait_ge(ones_ready, 2)
            pool.wait_ge(vec_in, 48)
            for b in range(B):
                pool.tensor_scalar(mcols[:, b, :], mcol8[:, b, :], 1.0, BIG, ALU.subtract, ALU.mult)\
                    .then_inc(mcols_done, 1)
                pool.wait_ge(mcols_done, b + 1)

            def unit(b, g, last):
                u = 4 * b + g
                if g == 0:
                    pool.wait_ge(mrow_in, 16 * b + 16)
                    if b:
                        pool.wait_ge(max_done, 4 * NT0 * b)
                    pool.tensor_scalar(mrow[:], mrow8[:], 1.0, BIG, ALU.subtract, ALU.mult).then_inc(mrow_ready, 1)
                    pool.wait_ge(mrow_ready, b + 1)
                if not isinstance(u, int) or u >= 2:
                    pool.wait_ge(pv_mm, NT0 * (u - 1))
                n = 0
                for half in range(2):
                    r = slice(64 * half, 64 * half + 64)
                    for src, dst in ((q_hi, qb_hi), (q_lo, qb_lo)):
                        pool.tensor_copy(dst[r, g % 2, :, half * P:half * P + P],
                                         src[r, 2 * g:2 * g + 2, bass.ds(b * P, P)]).then_inc(qb_ready, 1)
                        n += 1
                        pool.wait_ge(qb_ready, 4 * u + n)
                if g == 0:
                    if b:
                        pool.wait_ge(exp_done, 4 * NT0 * b)
                    pool.tensor_copy(mcol[:], mcols[:, b, :]).then_inc(mcol_ready, 1)
                    pool.wait_ge(mcol_ready, b + 1)

            for g in range(QUADS):
                unit(0, g, False)
            for b in range(1, B):
                for g in range(QUADS):
                    unit(b, g, False)

        @block.scalar
        def _(act):
            act.wait_ge(vec_in, 48)

            def norm_context(bb, first):
                for j in range(4):
                    act.wait_ge(var_ready, 4 * bb + j + 1)
                    act.activation(sd[:], va[:], ACT.Sqrt).then_inc(sd_ready, 1)
                    for c in range(C):
                        k = 4 * j + c
                        act.wait_ge(ln_tp, 16 * bb + k + 1)
                        if not (first and k < 2):
                            act.wait_ge(xlo_done, 16 * bb + k - 1)
                        act.activation(xf[:, k % 2, :], ps[:, 6 + k % 2, :], ACT.Identity, bias=bx[:, c:c + 1],
                                       scale=gx[:, c:c + 1]).then_inc(ln_evac, 1)
                        act.wait_ge(ln_evac, 16 * bb + k + 1)
                        act.activation(x_hi[:, c, j * 512:(j + 1) * 512], xf[:, k % 2, :], ACT.Copy)\
                           .then_inc(xhi_done, 1)

            def project(bb, gg, first, s):
                pu = 4 * bb + gg
                n = NT0 * pu + s
                j = s // 4
                G = G0 * pu + j
                if s == 0 and not first and not (isinstance(pu, int) and pu < 2):
                    act.wait_ge(pv_mm, NT0 * (pu - 1))
                if s % 4 == 0:
                    if not (isinstance(G, int) and G < 2):
                        act.wait_ge(kt_tp, 2 * (G - 1))
                    if not (isinstance(G, int) and G < 1):
                        act.wait_ge(ss_done, G)
                act.wait_ge(proj_mm, n + 1)
                bank = bank_p(gg, s)
                kp = (G0 * gg + j) % 2
                act.activation(kraw[:, kp, s % 4, :], ps[:, bank, 0:256], ACT.Copy)
                act.activation(sq[:, s % 4, :], ps[:, bank, 0:256], ACT.Square)
                act.activation(v[:, gg % 2, s, :, 0:DH0], heads(ps[:, bank, 256:512], DH0), ACT.Copy)\
                   .then_inc(vhi_done, 1)
                for kind, j, pr in after[s]:
                    G = G0 * pu + j
                    if kind == "norm":
                        act.wait_ge(ms_ready, G + 1)
                        act.activation(sdk[:, 0:4 * size[j]], ss[:, 0:4 * size[j]], ACT.Sqrt).then_inc(ksd_ready, 1)
                    elif kind == "turn":
                        act.wait_ge(kt_tp, 2 * G + pr + 1)
                        act.activation(k_hi[:, gg % 2, pr, j * 512:j * 512 + P * size[j]],
                                       ps[:, KT, 0:P * size[j]], ACT.Copy).then_inc(kthi_done, 1)

            def first():
                norm_context(0, True)
                for s in range(NT0):
                    project(0, 0, True, s)

            def unit(b, g, last):
                u = 4 * b + g
                if not last:
                    bb, gg = (b, g + 1) if g < 3 else (b + 1, 0)
                    if g == 3:
                        norm_context(bb, False)
                    for s in range(NT0):
                        project(bb, gg, False, s)
                if g == 0:
                    act.wait_ge(mcol_ready, b + 1)
                for s in range(NT0):
                    n = NT0 * u + s
                    act.wait_ge(s_mm, n + 1)
                    if s >= 2 or not (isinstance(u, int) and u == 0):
                        act.wait_ge(plo_done, n - 1)
                    bias = {"bias": mcol[:, s:s + 1]} if s < NT else {}
                    act.activation(p32[:, (NT0 * g + s) % 2, :], ps[:, (NT0 * g + s) % 2, :], ACT.Exp, **bias)\
                       .then_inc(exp_done, 1)
                act.wait_ge(pv_mm, NT0 * (u + 1))
                if not (isinstance(u, int) and u == 0):
                    act.wait_ge(ao_ready, u)
                act.activation(o32[:].rearrange("p h d -> p (h d)"), ps[:, PV, 0:4 * (DH0 + 1)], ACT.Copy)\
                   .then_inc(o_evac, 1)

            schedule(act, first, unit)

        @block.vector
        def _(dve):
            step = Steps(dve, dve_step)

            def norm_context(bb, first):
                if not first:
                    dve.wait_ge(proj_mm, 4 * NT0 * bb)
                for j in range(4):
                    dve.wait_ge(ctx_in, 64 * bb + 16 * j + 16)
                    for i in range(4):
                        last = dve.bn_stats(st[:, i, :], xn[:, i, :])
                    step(last)
                    for i in range(4):
                        last = dve.bn_aggr(mv[:, i, :], st[:, i, :])
                    step(last)
                    dve.tensor_scalar(va[:], mv[:, :, 1], 1e-5, None, ALU.add).then_inc(var_ready, 1)
                    dve.wait_ge(sd_ready, 4 * bb + j + 1)
                    step(dve.reciprocal(rstd[:], sd[:]))
                    for i in range(4):
                        dve.tensor_scalar(xn[:, i, :], xn[:, i, :], mv[:, i, 0:1], rstd[:, i:i + 1],
                                          ALU.subtract, ALU.mult).then_inc(xn_ready, 1)
                    for c in range(C):
                        k = 4 * j + c
                        dve.wait_ge(xhi_done, 16 * bb + k + 1)
                        dve.tensor_tensor(x_lo[:, c, j * 512:(j + 1) * 512], xf[:, k % 2, :],
                                          x_hi[:, c, j * 512:(j + 1) * 512], ALU.subtract).then_inc(xlo_done, 1)

            def project(bb, gg, s):
                pu = 4 * bb + gg
                n = NT0 * pu + s
                bank = bank_p(gg, s)
                dve.wait_ge(vhi_done, n + 1)
                vp = v[:, gg % 2, s]
                dve.tensor_tensor(vp[:, :, DH0 + 1:VW], heads(ps[:, bank, 256:512], DH0), vp[:, :, 0:DH0],
                                  ALU.subtract).then_inc(vlo_done, 1)
                for kind, j, pr in after[s]:
                    G = G0 * pu + j
                    w = 4 * size[j]
                    kp = (G0 * gg + j) % 2
                    if kind == "sum":
                        dve.tensor_reduce(ss[:, 0:w], sq[:, 0:size[j], :].rearrange("p i (h d) -> p (i h) d", d=DH0),
                                          AX.X, ALU.add).then_inc(ss_done, 1)
                        dve.wait_ge(ss_done, G + 1)
                        dve.tensor_scalar(ss[:, 0:w], ss[:, 0:w], 1.0 / DH0, 1e-16, ALU.mult, ALU.max)\
                           .then_inc(ms_ready, 1)
                    elif kind == "norm":
                        dve.wait_ge(ksd_ready, G + 1)
                        step(dve.reciprocal(rn[:, 0:w], sdk[:, 0:w]))
                        kr = kraw[:, kp, 0:size[j], :].rearrange("p i (h d) -> p (i h) d", d=DH0)
                        dve.tensor_tensor(kr, kr, per_head(rn[:, 0:w], w, DH0), ALU.mult).then_inc(kn_ready, 1)
                    else:
                        dve.wait_ge(kthi_done, 2 * G + pr + 1)
                        cols = slice(j * 512, j * 512 + P * size[j])
                        dve.tensor_tensor(k_lo[:, gg % 2, pr, cols], ps[:, KT, 0:P * size[j]],
                                          k_hi[:, gg % 2, pr, cols], ALU.subtract).then_inc(ktlo_done, 1)

            def maxima(b, g, k):
                u = 4 * b + g
                if k < 16:
                    h, kt = k // 4, k % 4
                    dve.wait_ge(max_mm, NT0 * u + k + 1)
                    if u or k:
                        dve.wait_ge(max_done, NT0 * u + k)
                    dve.tensor_tensor_reduce(junk[:], ps[:, bank_m(g, k), :], mrow[:, kt * 512:(kt + 1) * 512], 1.0,
                                             -3e38, ALU.add, ALU.max, mx[:, h, kt:kt + 1]).then_inc(max_done, 1)
                else:
                    dve.wait_ge(max_mm, NT0 * u + k + 1)
                    dve.tensor_reduce(mx[:, :, 4], heads(ps[:, bank_m(g, k), :], P), AX.X, ALU.max)\
                       .then_inc(max_done, 1)

            def first():
                norm_context(0, True)
                for s in range(NT0):
                    project(0, 0, s)

            def unit(b, g, last):
                u = 4 * b + g
                bb, gg = (b, g + 1) if g < 3 else (b + 1, 0)
                if g == 3 and not last:
                    norm_context(bb, False)
                if g == 0:
                    dve.wait_ge(mrow_ready, b + 1)
                for s in range(NT0):
                    if not last:
                        project(bb, gg, s)
                    maxima(b, g, s)
                dve.wait_ge(max_done, NT0 * (u + 1))
                step(dve.tensor_reduce(m4[:], mx[:], AX.X, ALU.max))
                if not (isinstance(u, int) and u == 0):
                    dve.wait_ge(s_mm, NT0 * u)
                for h in range(4):
                    dve.tensor_scalar(Dg[:, h, :], identb[:], m4[:, h:h + 1], -1.0, ALU.mult, ALU.mult)\
                       .then_inc(d_ready, 1)
                for s in range(NT0):
                    n = NT0 * u + s
                    par = (NT0 * g + s) % 2
                    dve.wait_ge(exp_done, n + 1)
                    if s >= 2 or not (isinstance(u, int) and u == 0):
                        dve.wait_ge(pv_mm, n - 1)
                    dve.tensor_copy(p_hi[:, par, :], p32[:, par, :]).then_inc(phi_done, 1)
                    dve.wait_ge(phi_done, n + 1)
                    dve.tensor_tensor(p_lo[:, par, :], p32[:, par, :], p_hi[:, par, :], ALU.subtract)\
                       .then_inc(plo_done, 1)
                dve.wait_ge(o_evac, u + 1)
                step(dve.reciprocal(rs[:], o32[:, :, DH0]))
                if not (isinstance(u, int) and u < 2):
                    dve.wait_ge(ao_out[g % 2], 16 * (2 * b + g // 2))
                dve.tensor_tensor(heads(ao[:, g % 2, :], DH0), o32[:, :, 0:DH0], per_head(rs[:], 4, DH0), ALU.mult)\
                   .then_inc(ao_ready, 1)

            first()
            for g in range(QUADS):
                unit(0, g, False)
            for b in range(1, B):
                for g in range(QUADS):
                    unit(b, g, (b, g) == (B - 1, QUADS - 1))

        @block.tensor
        def _(pe):
            def norm_context(bb, first):
                for j in range(4):
                    pe.wait_ge(xn_ready, 16 * bb + 4 * j + 4)
                    for c in range(C):
                        k = 4 * j + c
                        if k >= 2:
                            pe.wait_ge(ln_evac, 16 * bb + k - 1)
                        elif not first:
                            pe.wait_ge(max_done, NT0 * (4 * bb - 1))
                        for i in range(4):
                            last = pe.transpose(ps[:, 6 + k % 2, i * P:(i + 1) * P], xn[:, i, c * P:(c + 1) * P],
                                                identf[:])
                        last.then_inc(ln_tp, 1)

            def project(bb, gg, s):
                pu = 4 * bb + gg
                n = NT0 * pu + s
                if gg == 0:
                    if s < NT:
                        pe.wait_ge(xlo_done, 16 * bb + 4 * (s // 4) + 4)
                    else:
                        pe.wait_ge(lat_in, 32 * bb + 32)
                if not (isinstance(n, int) and n < 2):
                    pe.wait_ge(vlo_done, n - 1)
                out = ps[:, bank_p(gg, s), :]
                tile = slice(s * P, (s + 1) * P)
                for c in range(C):
                    pe.matmul(out, x_hi[:, c, tile], w_hi[:, c, gg, :], start=(c == 0), stop=False)
                    pe.matmul(out, x_hi[:, c, tile], w_lo[:, c, gg, :], start=False, stop=False)
                    last = pe.matmul(out, x_lo[:, c, tile], w_hi[:, c, gg, :], start=False, stop=(c == C - 1))
                last.then_inc(proj_mm, 1)
                for kind, j, pr in after[s]:
                    if kind == "turn":
                        G = G0 * pu + j
                        pe.wait_ge(kn_ready, G + 1)
                        if not (isinstance(G, int) and 2 * G + pr == 0):
                            pe.wait_ge(ktlo_done, 2 * G + pr)
                        for i in range(size[j]):
                            last = pe.transpose(ps[:, KT, i * P:(i + 1) * P],
                                                kraw[:, (G0 * gg + j) % 2, i, pr * P:(pr + 1) * P], identf[:])
                        last.then_inc(kt_tp, 1)

            def maxima(b, g, k, last):
                u = 4 * b + g
                if k == 0:
                    pe.wait_ge(qb_ready, 4 * (u + 1))
                    pe.wait_ge(ktlo_done, 2 * G0 * (u + 1))
                    pe.wait_ge(ln_evac, 16 * (b + 2) if g == 3 and not last else 16 * (b + 1))
                n = NT0 * u + k
                if not (isinstance(n, int) and n < 2):
                    pe.wait_ge(max_done, n - 1)
                out = ps[:, bank_m(g, k), :]
                if k < 16:
                    h, kt = k // 4, k % 4
                    mm = pe.matmul(out, qb_hi[:, g % 2, h // 2, (h % 2) * P:(h % 2 + 1) * P],
                                     k_hi[:, g % 2, h // 2, kt * 512:(kt + 1) * 512], start=True, stop=True)
                else:
                    for h in range(4):
                        mm = pe.matmul(out[:, h * P:(h + 1) * P],
                                         qb_hi[:, g % 2, h // 2, (h % 2) * P:(h % 2 + 1) * P],
                                         k_hi[:, g % 2, h // 2, S2:S0], start=True, stop=True)
                mm.then_inc(max_mm, 1)

            def scores(b, g, s):
                u = 4 * b + g
                n = NT0 * u + s
                if s == 0:
                    pe.wait_ge(d_ready, 4 * (u + 1))
                if not (isinstance(n, int) and n < 2):
                    pe.wait_ge(exp_done, n - 1)
                out = ps[:, (NT0 * g + s) % 2, :]
                tile = slice(s * P, (s + 1) * P)
                pe.matmul(out, onesb[:], Dg[:].rearrange("p h q -> p (h q)"), start=True, stop=False)
                for pr in range(2):
                    o = out[:, pr * 256:(pr + 1) * 256]
                    pe.matmul(o, k_hi[:, g % 2, pr, tile], qb_hi[:, g % 2, pr, :], start=False, stop=False)
                    pe.matmul(o, k_hi[:, g % 2, pr, tile], qb_lo[:, g % 2, pr, :], start=False, stop=False)
                    last = pe.matmul(o, k_lo[:, g % 2, pr, tile], qb_hi[:, g % 2, pr, :], start=False, stop=(pr == 1))
                last.then_inc(s_mm, 1)

            def values(b, g, s):
                u = 4 * b + g
                n = NT0 * u + s
                if s == 0:
                    pe.wait_ge(vlo_done, NT0 * (u + 1))
                    pe.wait_ge(ones_ready, 2)
                    if not (isinstance(u, int) and u == 0):
                        pe.wait_ge(o_evac, u)
                pe.wait_ge(plo_done, n + 1)
                par = (NT0 * g + s) % 2
                for h in range(4):
                    vh = v[:, g % 2, s, h]
                    o = ps[:, PV, h * (DH0 + 1):(h + 1) * (DH0 + 1)]
                    ph, pl = p_hi[:, par, h * P:(h + 1) * P], p_lo[:, par, h * P:(h + 1) * P]
                    pe.matmul(o, ph, vh[:, 0:DH0 + 1], start=(s == 0 and h == 0), stop=False, skip_group_check=True)
                    pe.matmul(o[:, 0:DH0], ph, vh[:, DH0 + 1:VW], start=False, stop=False, skip_group_check=True)
                    last = pe.matmul(o, pl, vh[:, 0:DH0 + 1], start=False, stop=(s == NT0 - 1 and h == 3),
                                     skip_group_check=True)
                last.then_inc(pv_mm, 1)

            def first():
                norm_context(0, True)
                for s in range(NT0):
                    project(0, 0, s)

            def unit(b, g, last):
                if g == 3 and not last:
                    norm_context(b + 1, False)
                for s in range(NT0):
                    if not last:
                        project(*((b, g + 1) if g < 3 else (b + 1, 0)), s)
                    maxima(b, g, s, last)
                scores(b, g, 0)
                for s in range(1, NT0):
                    scores(b, g, s)
                    values(b, g, s - 1)
                values(b, g, NT0 - 1)

            schedule(pe, first, unit)


class Turn:

    def __init__(self, sem, tag, chunks, banks):
        self.chunks, self.banks = chunks, banks
        self.turned, self.copied = sem(f"{tag}_turned"), sem(f"{tag}_copied")

    def tensor(self, pe, ps, src, ident):
        nb = len(self.banks)
        for c in range(self.chunks):
            if c >= nb:
                pe.wait_ge(self.copied, c - nb + 1)
            for b in range(B):
                last = pe.transpose(ps[:, self.banks[c % nb], b * P:(b + 1) * P], src[:, b, c * P:(c + 1) * P],
                                    ident[:])
            last.then_inc(self.turned, 1)

    def scalar(self, act, ps, dst):
        for c in range(self.chunks):
            act.wait_ge(self.turned, c + 1)
            act.activation(dst[:, c, :], ps[:, self.banks[c % len(self.banks)], :], ACT.Copy)\
               .then_inc(self.copied, 1)


def cross0_finish(nc, t, X, sb, sem):
    ps, identf = t["ps"], t["identf"]
    CI = INNER // P
    ao = sb("f0_ao", [P, B, INNER], F32)
    aot = sb("f0_aot", [P, CI, TOK], F32)
    wo = sb("f0_wo", [P, CI, D], F32)
    bo = sb("f0_bo", [P, D], F32)
    turn = Turn(sem, "f0", CI, [0, 1, 2, 3])
    x_in, ao_in, w_in, b_in = sem("f0_x_in"), sem("f0_ao_in"), sem("f0_w_in"), sem("f0_b_in")
    mm, xb, done = sem("f0_mm"), sem("f0_xb"), sem("f0_done")

    with nc.Block() as block:

        @block.sync
        def _(sp):
            sp.dma_start(ao[:], t["ao_d"].rearrange("b p n -> p b n")).then_inc(ao_in, 16)
            sp.dma_start(wo[:], t["L0_xattn_Wout"].rearrange("(c p) n -> p c n", p=P)).then_inc(w_in, 16)
            sp.dma_start(X[:], t["x"].rearrange("b p d -> p b d")).then_inc(x_in, 16)
            sp.dma_start(bo[:], row(t["L0_xattn_bout"], D)).then_inc(b_in, 16)

        @block.scalar
        def _(act):
            turn.scalar(act, ps, aot)

        @block.vector
        def _(dve):
            dve.wait_ge(x_in, 16)
            dve.wait_ge(b_in, 16)
            for b in range(B):
                dve.tensor_tensor(X[:, b, :], X[:, b, :], bo[:], ALU.add).then_inc(xb, 1)
            dve.wait_ge(xb, B)
            for b in range(B):
                dve.wait_ge(mm, b + 1)
                dve.tensor_tensor(X[:, b, :], X[:, b, :], ps[:, 4 + b, :], ALU.add).then_inc(done, 1)
            dve.wait_ge(done, B)

        @block.tensor
        def _(pe):
            pe.wait_ge(ao_in, 16)
            turn.tensor(pe, ps, ao, identf)
            pe.wait_ge(w_in, 16)
            pe.wait_ge(turn.copied, CI)
            for b in range(B):
                for c in range(CI):
                    last = pe.matmul(ps[:, 4 + b, :], aot[:, c, b * P:(b + 1) * P], wo[:, c, :],
                                     start=(c == 0), stop=(c == CI - 1))
                last.then_inc(mm, 1)


HS, KVS, DS = 8, 2, 128
GS = HS // KVS
RD = DS // 4


def self0(nc, t, X, sb, sem):
    ps, identf = t["ps"], t["identf"]
    NQ = HS * DS
    Hn = sb("s0_h", [P, B, D], F32)
    HT = sb("s0_ht", [P, C, TOK], F32)
    wq = sb("s0_wq", [P, C, 2 * NQ], F32)
    wkv = sb("s0_wkv", [P, C, 512], F32)
    q = sb("s0_q", [P, B, NQ], F32)
    gate = sb("s0_gate", [P, B, NQ], F32)
    kv = sb("s0_kv", [P, B, 512], F32)
    qT = sb("s0_qt", [P, HS, TOK], F32)
    kT = sb("s0_kt", [P, KVS, TOK], F32)
    cs = sb("s0_cs", [P, 2, RD], F32)
    r1 = sb("s0_r1", [P, B * HS, RD], F32)
    r2 = sb("s0_r2", [P, B * HS, RD], F32)
    p32 = sb("s0_p", [P, 2, 512], F32)
    pT = sb("s0_pt", [P, 2, 512], F32)
    mx = sb("s0_mx", [P, 2, GS], F32)
    nm = sb("s0_nm", [P, 2, GS], F32)
    sums = sb("s0_sum", [P, 2, GS], F32)
    rs = sb("s0_rs", [P, 2, GS], F32)
    norm = Norm(sb, sem, "s0n")
    turn_h = Turn(sem, "s0th", C, [0, 1, 2, 3])
    turn_q = Turn(sem, "s0tq", HS, [0, 1, 2, 3])
    turn_k = Turn(sem, "s0tk", KVS, [4, 5])
    turn_o = Turn(sem, "s0to", HS, [0, 1, 2, 3])
    wq_in, wkv_in, cs_in, wo_in = sem("s0_wq_in"), sem("s0_wkv_in"), sem("s0_cs_in"), sem("s0_wo_in")
    dve_step = sem("s0_dve")
    proj, cp, rot = sem("s0_proj"), sem("s0_cp"), sem("s0_rot")
    s_mm, nm_ready, e_done, p_turn, pt_cp, pv_mm, og = (sem("s0_s"), sem("s0_nmr"), sem("s0_e"), sem("s0_ptn"),
                                                        sem("s0_ptc"), sem("s0_pv"), sem("s0_og"))
    o_mm, done, g_mul = sem("s0_o"), sem("s0_done"), sem("s0_gmul")
    wo = wq[:, 0:2, :].rearrange("p a (c n) -> p (a c) n", n=D)
    NP = 5
    U = B * KVS

    with nc.Block() as block:

        @block.sync
        def _(sp):
            sp.dma_start(wq[:], t["L0_attn_Wq"].rearrange("(c p) n -> p c n", p=P)).then_inc(wq_in, 16)
            sp.dma_start(wkv[:, :, 0:256], t["L0_attn_Wk"].rearrange("(c p) n -> p c n", p=P)).then_inc(wkv_in, 16)
            sp.dma_start(wkv[:, :, 256:512], t["L0_attn_Wv"].rearrange("(c p) n -> p c n", p=P)).then_inc(wkv_in, 16)
            sp.dma_start(cs[:], t["rope"]).then_inc(cs_in, 16)
            sp.wait_ge(proj, NP * B)
            sp.dma_start(wo, t["L0_attn_Wo"].rearrange("(c p) n -> p c n", p=P)).then_inc(wo_in, 16)

        @block.scalar
        def _(act):
            norm.scalar(act)
            turn_h.scalar(act, ps, HT)
            for b in range(B):
                for n in range(NP):
                    k = NP * b + n
                    act.wait_ge(proj, k + 1)
                    src = ps[:, 4 + k % 4, :]
                    if n < 2:
                        act.activation(q[:, b, n * 512:(n + 1) * 512], src, ACT.Copy).then_inc(cp, 1)
                    elif n < 4:
                        act.activation(gate[:, b, (n - 2) * 512:(n - 1) * 512], src, ACT.Silu).then_inc(cp, 1)
                    else:
                        act.activation(kv[:, b, :], src, ACT.Copy).then_inc(cp, 1)
            turn_k.scalar(act, ps, kT)
            turn_q.scalar(act, ps, qT)

            def turned(u):
                act.wait_ge(p_turn, u + 1)
                if u >= 2:
                    act.wait_ge(pv_mm, u - 1)
                act.activation(pT[:, u % 2, :], ps[:, 2 + u % 2, :], ACT.Copy).then_inc(pt_cp, 1)

            for u in range(U):
                act.wait_ge(nm_ready, u + 1)
                if u >= 2:
                    act.wait_ge(p_turn, u - 1)
                    act.wait_ge(og, u - 1)
                for g in range(GS):
                    act.activation(p32[:, u % 2, g * P:(g + 1) * P], ps[:, u % 2, g * P:(g + 1) * P], ACT.Exp,
                                   bias=nm[:, u % 2, g:g + 1], scale=DS ** -0.5,
                                   accum_out=sums[:, u % 2, g:g + 1]).then_inc(e_done, 1)
                if u >= 1:
                    turned(u - 1)
            turned(U - 1)
            turn_o.scalar(act, ps, qT)

        @block.vector
        def _(dve):
            step = Steps(dve, dve_step)
            norm.vector(dve, step, Hn, X)

            def rotate(view, n):
                a, b2 = r1[:, 0:n, :], r2[:, 0:n, :]
                half = RD // 2
                cos = cs[:, 0:1, :].to_broadcast([P, n, RD])
                dve.tensor_tensor(a, view[:, :, 0:RD], cos, ALU.mult)
                dve.tensor_tensor(b2[:, :, 0:half], view[:, :, half:RD],
                                  cs[:, 1:2, 0:half].to_broadcast([P, n, half]), ALU.mult)
                step(dve.tensor_tensor(b2[:, :, half:RD], view[:, :, 0:half],
                                       cs[:, 1:2, half:RD].to_broadcast([P, n, half]), ALU.mult))
                return dve.tensor_tensor(view[:, :, 0:RD], a, b2, ALU.add)

            dve.wait_ge(cs_in, 16)
            dve.wait_ge(cp, NP * B)
            for b in range(B):
                step(rotate(heads(kv[:, b, 0:KVS * DS], DS), KVS))
            rotate(q[:].rearrange("p b (h d) -> p (b h) d", d=DS), B * HS).then_inc(rot, 1)

            def output(u):
                b, k = u // KVS, u % KVS
                dve.wait_ge(pv_mm, u + 1)
                step(dve.reciprocal(rs[:, u % 2, :], sums[:, u % 2, :]))
                o = heads(q[:, b, k * 512:(k + 1) * 512], DS)
                step(dve.tensor_tensor(o, heads(ps[:, 4 + u % 2, :], DS), per_head(rs[:, u % 2, :], GS, DS), ALU.mult))
                dve.tensor_tensor(q[:, b, k * 512:(k + 1) * 512], q[:, b, k * 512:(k + 1) * 512],
                                  gate[:, b, k * 512:(k + 1) * 512], ALU.mult).then_inc(og, 1)

            for u in range(U):
                dve.wait_ge(s_mm, u + 1)
                if u >= 2:
                    dve.wait_ge(e_done, GS * (u - 1))
                step(dve.tensor_reduce(mx[:, u % 2, :], heads(ps[:, u % 2, :], P), AX.X, ALU.max))
                dve.tensor_scalar(nm[:, u % 2, :], mx[:, u % 2, :], -DS ** -0.5, None, ALU.mult).then_inc(nm_ready, 1)
                if u >= 1:
                    output(u - 1)
            output(U - 1)
            for b in range(B):
                dve.wait_ge(o_mm, b + 1)
                dve.tensor_tensor(X[:, b, :], X[:, b, :], ps[:, 4 + b, :], ALU.add).then_inc(done, 1)
            dve.wait_ge(done, B)

        @block.tensor
        def _(pe):
            pe.wait_ge(norm.done, B)
            turn_h.tensor(pe, ps, Hn, identf)
            pe.wait_ge(turn_h.copied, C)
            pe.wait_ge(wq_in, 16)
            pe.wait_ge(wkv_in, 32)
            for b in range(B):
                for n in range(NP):
                    k = NP * b + n
                    if k >= 4:
                        pe.wait_ge(cp, k - 3)
                    for c in range(C):
                        w = wq[:, c, n * 512:(n + 1) * 512] if n < 4 else wkv[:, c, :]
                        last = pe.matmul(ps[:, 4 + k % 4, :], HT[:, c, b * P:(b + 1) * P], w,
                                         start=(c == 0), stop=(c == C - 1))
                    last.then_inc(proj, 1)
            pe.wait_ge(rot, 1)
            turn_k.tensor(pe, ps, kv, identf)
            turn_q.tensor(pe, ps, q, identf)
            pe.wait_ge(turn_q.copied, HS)
            pe.wait_ge(turn_k.copied, KVS)

            def scores(u):
                b, k = u // KVS, u % KVS
                if u >= 2:
                    pe.wait_ge(e_done, GS * (u - 1))
                for g in range(GS):
                    last = pe.matmul(ps[:, u % 2, g * P:(g + 1) * P], qT[:, k * GS + g, b * P:(b + 1) * P],
                                     kT[:, k, b * P:(b + 1) * P], start=True, stop=True)
                last.then_inc(s_mm, 1)

            def turn_p(u):
                pe.wait_ge(e_done, GS * (u + 1))
                if u >= 2:
                    pe.wait_ge(pt_cp, u - 1)
                for g in range(GS):
                    last = pe.transpose(ps[:, 2 + u % 2, g * P:(g + 1) * P], p32[:, u % 2, g * P:(g + 1) * P],
                                        identf[:])
                last.then_inc(p_turn, 1)

            def values(u):
                b, k = u // KVS, u % KVS
                pe.wait_ge(pt_cp, u + 1)
                if u >= 2:
                    pe.wait_ge(og, u - 1)
                for g in range(GS):
                    last = pe.matmul(ps[:, 4 + u % 2, g * P:(g + 1) * P], pT[:, u % 2, g * P:(g + 1) * P],
                                     kv[:, b, (KVS + k) * DS:(KVS + k + 1) * DS], start=True, stop=True)
                last.then_inc(pv_mm, 1)

            for i in range(U + 2):
                if i < U:
                    scores(i)
                if 1 <= i <= U:
                    turn_p(i - 1)
                if i >= 2:
                    values(i - 2)
            pe.wait_ge(og, U)
            turn_o.tensor(pe, ps, q, identf)
            pe.wait_ge(turn_o.copied, HS)
            pe.wait_ge(wo_in, 16)
            for b in range(B):
                for c in range(HS):
                    last = pe.matmul(ps[:, 4 + b, :], qT[:, c, b * P:(b + 1) * P], wo[:, c, :],
                                     start=(c == 0), stop=(c == HS - 1))
                last.then_inc(o_mm, 1)


E, HID = 16, 1024
CH = HID // P


def experts(nc, t, X, sb, sem):
    ps, identf = t["ps"], t["identf"]
    Hn = sb("e_h", [P, B, D], F32)
    HT = sb("e_ht", [P, C, TOK], F32)
    h_hi = sb("e_hhi", [P, C, TOK], BF16)
    h_lo = sb("e_hlo", [P, C, TOK], BF16)
    wst = sb("e_wst", [P, 2, 4096], F32)
    w_hi = sb("e_whi", [P, 2, 2, 4096], BF16)
    w_lo = sb("e_wlo", [P, 2, 2, 4096], BF16)
    b1 = sb("e_b1", [P, E, CH], F32)
    g32 = sb("e_g", [P, 2, TOK], F32)
    g_hi = sb("e_ghi", [P, CH, TOK], BF16)
    g_lo = sb("e_glo", [P, CH, TOK], BF16)
    wr = sb("e_wr", [P, C, E], F32)
    br = sb("e_br", [P, E], F32)
    b2 = sb("e_b2", [E, D], F32)
    cT = sb("e_ct", [E, TOK], F32)
    lg = sb("e_lg", [P, B, E], F32)
    pr = sb("e_pr", [P, B, E], F32)
    rest = sb("e_rest", [P, B, E], F32)
    comb = sb("e_comb", [P, B, E], F32)
    m8 = sb("e_m8", [P, B, 8], F32)
    v1 = sb("e_v1", [P, B, 4], F32)
    norm = Norm(sb, sem, "en")
    turn = Turn(sem, "et", C, [0, 1, 2, 3])
    small_in = sem("e_small_in")
    w_in = [sem("e_w1_in"), sem("e_w2_in")]
    hi_done, lo_done, whi, wlo = sem("e_hi"), sem("e_lo"), sem("e_whi_d"), sem("e_wlo_d")
    dve_step = sem("e_dve")
    lg_mm, nm_ready, ex_done, comb_ready, ct_turn, ct_ready, b2_mm = (
        sem("e_lg"), sem("e_nm"), sem("e_ex"), sem("e_comb_r"), sem("e_ctt"), sem("e_ctr"), sem("e_b2mm"))
    up_mm, gelu, ghi, glo, down_mm, y_done = (sem("e_up"), sem("e_gelu"), sem("e_ghi_d"), sem("e_glo_d"),
                                              sem("e_down"), sem("e_y"))
    w1_d = t["L0_ffn_W1"].rearrange("e (c p) n -> e p c n", p=P)
    w2_d = t["L0_ffn_W2"].rearrange("e (c p) n -> e p c n", p=P)

    def w1(w, par):
        return w[:, par, 0, :].rearrange("p (c n) -> p c n", n=HID)

    def w2(w, par):
        return w[:, par, 1, :].rearrange("p (c n) -> p c n", n=D)

    def up_bank(par, m):
        return (CH * par + m) % 4

    def over_experts(eng, one):
        for par in range(2):
            one(par, par)
        with eng.Fori(1, E // 2) as i:
            for par in range(2):
                one(2 * i + par, par)

    with nc.Block() as block:

        @block.sync
        def _(sp):
            sp.dma_start(wr[:], t["L0_ffn_Wr"].rearrange("(c p) e -> p c e", p=P)).then_inc(small_in, 16)
            sp.dma_start(br[:], row(t["L0_ffn_br"], E)).then_inc(small_in, 16)
            sp.dma_start(b2[:], t["L0_ffn_b2"]).then_inc(small_in, 16)
            sp.dma_start(b1[:], t["moe_b1_col"]).then_inc(small_in, 16)

            def one(e, par):
                for half, src in ((0, w1_d), (1, w2_d)):
                    if not isinstance(e, int) or e > 0:
                        sp.wait_ge(wlo, 2 * e - 1 + half)
                    n = HID if half == 0 else D
                    sp.dma_start(wst[:, half, :].rearrange("p (c n) -> p c n", n=n), src[e]).then_inc(w_in[half], 16)

            over_experts(sp, one)

        @block.scalar
        def _(act):
            norm.scalar(act)
            turn.scalar(act, ps, HT)
            act.wait_ge(turn.copied, C)
            for c in range(C):
                act.activation(h_hi[:, c, :], HT[:, c, :], ACT.Copy).then_inc(hi_done, 1)

            def split(e, par):
                for half in range(2):
                    if not isinstance(e, int) or e > 1:
                        act.wait_ge(down_mm, B * (e - 1))
                    act.wait_ge(w_in[half], 16 * (e + 1))
                    act.activation(w_hi[:, par, half, :], wst[:, half, :], ACT.Copy).then_inc(whi, 1)

            split(0, 0)
            act.wait_ge(nm_ready, 1)
            for b in range(B):
                act.activation(pr[:, b, :], lg[:, b, :], ACT.Exp, bias=v1[:, b, 0:1],
                               accum_out=v1[:, b, 1:2]).then_inc(ex_done, 1)
            act.wait_ge(ct_turn, 1)
            act.activation(cT[:], ps[0:E, 1, :], ACT.Copy).then_inc(ct_ready, 1)
            act.wait_ge(small_in, 64)

            def one(e, par):
                for m in range(CH):
                    n = CH * e + m
                    act.wait_ge(up_mm, n + 1)
                    if not isinstance(n, int) or n >= 2:
                        act.wait_ge(glo, n - 1)
                    if m == 0 and (not isinstance(e, int) or e > 0):
                        act.wait_ge(down_mm, B * e)
                    act.activation(g32[:, m % 2, :], ps[:, up_bank(par, m), :],
                                   ACT.Gelu, bias=b1[:, e, m:m + 1]).then_inc(gelu, 1)
                    act.wait_ge(gelu, n + 1)
                    act.activation(g_hi[:, m, :], g32[:, m % 2, :], ACT.Copy).then_inc(ghi, 1)
                    if m == 1 and par == 0:
                        split(e + 1, 1)
                    if m == 1 and par == 1:
                        split_next(e + 1)

            def split_next(e):
                if isinstance(e, int) and e == E:
                    return
                split(e, 0)

            for par in range(2):
                one(par, par)
            with act.Fori(1, E // 2 - 1) as i:
                for par in range(2):
                    one(2 * i + par, par)
            for par in range(2):
                one(E - 2 + par, par)

        @block.vector
        def _(dve):
            step = Steps(dve, dve_step)
            norm.vector(dve, step, Hn, X)
            for c in range(C):
                dve.wait_ge(hi_done, c + 1)
                dve.tensor_tensor(h_lo[:, c, :], HT[:, c, :], h_hi[:, c, :], ALU.subtract).then_inc(lo_done, 1)

            def split(e, par):
                for half in range(2):
                    dve.wait_ge(whi, 2 * e + half + 1)
                    dve.tensor_tensor(w_lo[:, par, half, :], wst[:, half, :], w_hi[:, par, half, :],
                                      ALU.subtract).then_inc(wlo, 1)

            split(0, 0)
            dve.wait_ge(lg_mm, 1)
            dve.wait_ge(small_in, 64)
            step(dve.tensor_tensor(lg[:], ps[:, 0, 0:B * E].rearrange("p (b e) -> p b e", e=E),
                                   br[:].unsqueeze(1).to_broadcast([P, B, E]), ALU.add))
            step(dve.tensor_reduce(v1[:, :, 0], lg[:], AX.X, ALU.max))
            dve.tensor_scalar(v1[:, :, 0], v1[:, :, 0], -1.0, None, ALU.mult).then_inc(nm_ready, 1)
            dve.wait_ge(ex_done, B)
            step(dve.reciprocal(v1[:, :, 3], v1[:, :, 1]))
            step(dve.tensor_tensor(pr[:], pr[:], per_head(v1[:, :, 3], B, E), ALU.mult))
            for b in range(B):
                last = dve.max(m8[:, b, :], pr[:, b, :])
            step(last)
            step(dve.tensor_tensor(v1[:, :, 2], m8[:, :, 0], m8[:, :, 1], ALU.add))
            step(dve.tensor_scalar(v1[:, :, 2], v1[:, :, 2], 1e-9, None, ALU.max))
            step(dve.reciprocal(v1[:, :, 3], v1[:, :, 2]))
            step(dve.memset(m8[:, :, 2:8], -1.0))
            for b in range(B):
                last = dve.match_replace(rest[:, b, :], m8[:, b, :], pr[:, b, :], 0.0)
            step(last)
            step(dve.tensor_tensor(comb[:], pr[:], rest[:], ALU.subtract))
            dve.tensor_tensor(comb[:], comb[:], per_head(v1[:, :, 3], B, E), ALU.mult).then_inc(comb_ready, 1)
            for b in range(B):
                last = dve.tensor_tensor(X[:, b, :], X[:, b, :], Hn[:, b, :], ALU.add)
            step(last)
            for b in range(B):
                dve.wait_ge(b2_mm, b + 1)
                dve.tensor_tensor(X[:, b, :], X[:, b, :], ps[:, 4 + b, :], ALU.add).then_inc(y_done, 1)

            def one(e, par, last=False):
                for m in range(CH):
                    n = CH * e + m
                    dve.wait_ge(ghi, n + 1)
                    dve.tensor_tensor(g_lo[:, m, :], g32[:, m % 2, :], g_hi[:, m, :], ALU.subtract).then_inc(glo, 1)
                    if m == 1 and not last:
                        split(e + 1, 1 - par)
                for b in range(B):
                    dve.wait_ge(down_mm, B * e + b + 1)
                    dve.wait_ge(y_done, B * (e + 1))
                    dve.scalar_tensor_tensor(X[:, b, :], ps[:, 4 + b, :], comb[:, b, bass.ds(e, 1)], X[:, b, :],
                                             ALU.mult, ALU.add).then_inc(y_done, 1)

            for par in range(2):
                one(par, par)
            with dve.Fori(1, E // 2 - 1) as i:
                for par in range(2):
                    one(2 * i + par, par)
            for par in range(2):
                one(E - 2 + par, par, par == 1)
            dve.wait_ge(y_done, B * (E + 1))

        @block.tensor
        def _(pe):
            pe.wait_ge(norm.done, B)
            turn.tensor(pe, ps, Hn, identf)
            pe.wait_ge(turn.copied, C)
            pe.wait_ge(small_in, 64)
            for b in range(B):
                for c in range(C):
                    last = pe.matmul(ps[:, 0, b * E:(b + 1) * E], HT[:, c, b * P:(b + 1) * P], wr[:, c, :],
                                     start=(c == 0), stop=(c == C - 1))
            last.then_inc(lg_mm, 1)
            pe.wait_ge(comb_ready, 1)
            for b in range(B):
                last = pe.transpose(ps[0:E, 1, b * P:(b + 1) * P], comb[:, b, :], identf[:])
            last.then_inc(ct_turn, 1)
            pe.wait_ge(ct_ready, 1)
            for b in range(B):
                pe.matmul(ps[:, 4 + b, :], cT[:, b * P:(b + 1) * P], b2[:], start=True, stop=True).then_inc(b2_mm, 1)
            pe.wait_ge(lo_done, C)

            def one(e, par):
                pe.wait_ge(wlo, 2 * e + 1)
                for m in range(CH):
                    n = CH * e + m
                    if not isinstance(n, int) or n >= 4:
                        pe.wait_ge(gelu, n - 3)
                    out = ps[:, up_bank(par, m), :]
                    cols = slice(m * P, (m + 1) * P)
                    for c in range(C):
                        pe.matmul(out, w1(w_hi, par)[:, c, cols], h_hi[:, c, :], start=(c == 0), stop=False)
                        pe.matmul(out, w1(w_hi, par)[:, c, cols], h_lo[:, c, :], start=False, stop=False)
                        last = pe.matmul(out, w1(w_lo, par)[:, c, cols], h_hi[:, c, :], start=False,
                                         stop=(c == C - 1))
                    last.then_inc(up_mm, 1)
                pe.wait_ge(wlo, 2 * e + 2)
                for b in range(B):
                    pe.wait_ge(y_done, B * e + b + 1)
                    cols = slice(b * P, (b + 1) * P)
                    for m in range(CH):
                        if b == 0:
                            pe.wait_ge(glo, CH * e + m + 1)
                        out = ps[:, 4 + b, :]
                        pe.matmul(out, g_hi[:, m, cols], w2(w_hi, par)[:, m, :], start=(m == 0), stop=False)
                        pe.matmul(out, g_hi[:, m, cols], w2(w_lo, par)[:, m, :], start=False, stop=False)
                        last = pe.matmul(out, g_lo[:, m, cols], w2(w_hi, par)[:, m, :], start=False,
                                         stop=(m == CH - 1))
                    last.then_inc(down_mm, 1)

            over_experts(pe, one)


H1, DH1 = 16, 32


def cross1_prepare(nc, t, X, keep, sb, sem):
    ps, identf = t["ps"], t["identf"]
    Hn = sb("c1_h", [P, B, D], F32)
    HT = sb("c1_ht", [P, C, TOK], F32)
    wq = sb("c1_wq", [P, C, D], F32)
    wst = sb("c1_wst", [P, 2, C, D], F32)
    bq = sb("c1_bq", [P, QUADS], F32)
    bqs = sb("c1_bqs", [P, QUADS], F32)
    q32 = sb("c1_q32", [P, QUADS, TOK], F32)
    norm = Norm(sb, sem, "c1n")
    turn = Turn(sem, "c1t", C, [0, 1, 2, 3])
    wq_in, wk_in, b_in, x_out = sem("c1_wq_in"), sem("c1_wk_in"), sem("c1_b_in"), sem("c1_x_out")
    dve_step, w_hi_done, w_lo_done = sem("c1_dve"), sem("c1_whi"), sem("c1_wlo")
    bq_ready, q_mm, q_cp, q_hi_done, q_lo_done = (sem("c1_bqr"), sem("c1_qmm"), sem("c1_qcp"), sem("c1_qhi"),
                                                  sem("c1_qlo"))

    with nc.Block() as block:

        @block.sync
        def _(sp):
            sp.dma_start(t["x_d"].rearrange("b p d -> p b d"), X[:]).then_inc(x_out, 16)
            sp.dma_start(wq[:], t["wqT1"].rearrange("(c p) n -> p c n", p=P)).then_inc(wq_in, 16)
            sp.dma_start(wst[:, 0], t["wkT1"].rearrange("(c p) n -> p c n", p=P)).then_inc(wk_in, 16)
            sp.dma_start(wst[:, 1], t["wvT1"].rearrange("(c p) n -> p c n", p=P)).then_inc(wk_in, 16)
            sp.dma_start(bq[:], t["L1_xattn_bq_col"]).then_inc(b_in, 16)
            sp.wait_ge(x_out, 16)

        @block.gpsimd
        def _(pool):
            for k in range(2):
                pool.wait_ge(w_hi_done, k + 1)
                if k:
                    pool.wait_ge(w_lo_done, k)
                pool.tensor_tensor(keep["w_lo"][:, k], wst[:, k], keep["w_hi"][:, k], ALU.subtract)\
                    .then_inc(w_lo_done, 1)

        @block.scalar
        def _(act):
            norm.scalar(act)
            turn.scalar(act, ps, HT)
            act.wait_ge(wk_in, 32)
            for k in range(2):
                act.activation(keep["w_hi"][:, k], wst[:, k], ACT.Copy).then_inc(w_hi_done, 1)
            act.wait_ge(bq_ready, 1)
            for g in range(QUADS):
                act.wait_ge(q_mm, g + 1)
                act.activation(q32[:, g, :], ps[:, 4 + g, :], ACT.Identity, bias=bqs[:, g:g + 1],
                               scale=DH1 ** -0.5).then_inc(q_cp, 1)
            act.wait_ge(q_cp, QUADS)
            for g in range(QUADS):
                act.activation(keep["q_hi"][:, g, :], q32[:, g, :], ACT.Copy).then_inc(q_hi_done, 1)

        @block.vector
        def _(dve):
            step = Steps(dve, dve_step)
            norm.vector(dve, step, Hn, X)
            dve.wait_ge(b_in, 16)
            dve.tensor_scalar(bqs[:], bq[:], DH1 ** -0.5, None, ALU.mult).then_inc(bq_ready, 1)
            for g in range(QUADS):
                dve.wait_ge(q_hi_done, g + 1)
                dve.tensor_tensor(keep["q_lo"][:, g, :], q32[:, g, :], keep["q_hi"][:, g, :], ALU.subtract)\
                   .then_inc(q_lo_done, 1)
            dve.wait_ge(q_lo_done, QUADS)

        @block.tensor
        def _(pe):
            pe.wait_ge(norm.done, B)
            turn.tensor(pe, ps, Hn, identf)
            pe.wait_ge(turn.copied, C)
            pe.wait_ge(wq_in, 16)
            for g in range(QUADS):
                for c in range(C):
                    last = pe.matmul(ps[:, 4 + g, :], wq[:, c, g * P:(g + 1) * P], HT[:, c, :],
                                     start=(c == 0), stop=(c == C - 1))
                last.then_inc(q_mm, 1)


def cross1_attend(nc, t, keep, sb, sem):
    ps, identb, onesb = t["ps"], t["identb"], t["onesb"]
    w_hi, w_lo, q_hi, q_lo = keep["w_hi"], keep["w_lo"], keep["q_hi"], keep["q_lo"]
    VW = 2 * DH1 + 1
    cT = sb("a1_ct", [P, C, 512], F32)
    c_hi = sb("a1_chi", [P, C, 512], BF16)
    c_lo = sb("a1_clo", [P, C, 512], BF16)
    k32 = sb("a1_k32", [P, 512], F32)
    k_hi = sb("a1_khi", [P, 2, QUADS, S2], BF16)
    k_lo = sb("a1_klo", [P, 2, QUADS, S2], BF16)
    v = sb("a1_v", [P, 2, NT, H1, VW], BF16)
    mst = sb("a1_mst", [P, 512], I32)
    keeprow = sb("a1_keeprow", [P, S2], BF16)
    biasrow = sb("a1_biasrow", [P, S2], BF16)
    mcol32 = sb("a1_mcol32", [P, B, NT], I32)
    kcol = sb("a1_kcol", [P, B, NT], F32)
    mcol = sb("a1_mcol", [P, NT], F32)
    some = sb("a1_some", [P, 1], F32)
    bk = sb("a1_bk", [P, QUADS], F32)
    bv = sb("a1_bv", [P, D], F32)
    qb_hi = sb("a1_qbhi", [P, 2, 512], BF16)
    qb_lo = sb("a1_qblo", [P, 2, 512], BF16)
    p32 = sb("a1_p32", [P, 2, 512], F32)
    p_hi = sb("a1_phi", [P, 2, 512], BF16)
    p_lo = sb("a1_plo", [P, 2, 512], BF16)
    junk = sb("a1_junk", [P, 512], BF16)
    mx = sb("a1_mx", [P, 4, 4], F32)
    m4 = sb("a1_m4", [P, 4], F32)
    Dg = sb("a1_d", [P, 4, P], BF16)
    o32 = sb("a1_o32", [P, 4, DH1 + 1], F32)
    rs = sb("a1_rs", [P, 4], F32)
    ao = sb("a1_ao", [P, 2, P], F32)

    vec_in, ct_in, mst_in = sem("a1_vec_in"), sem("a1_ct_in"), sem("a1_mst_in")
    chi_done, clo_done = sem("a1_chi_d"), sem("a1_clo_d")
    proj_mm, k_ready, khi_done, klo_done, vhi_done, vlo_done = (
        sem("a1_proj"), sem("a1_k"), sem("a1_khi_d"), sem("a1_klo_d"), sem("a1_vhi_d"), sem("a1_vlo_d"))
    keep_cv, mcol_ready, kcol_ready = sem("a1_keepcv"), sem("a1_mcolr"), sem("a1_kcolr")
    zero_done, ones_ready, qb_ready = sem("a1_zero"), sem("a1_onesr"), sem("a1_qbr")
    max_mm, max_done, d_ready = sem("a1_maxmm"), sem("a1_maxd"), sem("a1_dr")
    s_mm, exp_done, phi_done, plo_done, pv_mm = sem("a1_s"), sem("a1_exp"), sem("a1_phid"), sem("a1_plod"), sem("a1_pv")
    o_evac, ao_ready = sem("a1_o"), sem("a1_aor")
    ao_out = [sem("a1_ao_out0"), sem("a1_ao_out1")]
    dve_step = sem("a1_dve")

    PV = 2
    PU = 8

    def bank_p(n):
        return 3 + n % 2

    def bank_m(n):
        return 5 + n % 3

    with nc.Block() as block:

        @block.sync
        def _(sp):
            sp.dma_start(bk[:], t["L1_xattn_bk_col"]).then_inc(vec_in, 16)
            sp.dma_start(bv[:], row(t["L1_xattn_bv"], D)).then_inc(vec_in, 16)
            sp.dma_start(mcol32[:], t["mask1_col"]).then_inc(vec_in, 16)

            def mask(b):
                for j in range(4):
                    n = 4 * b + j
                    if n >= 1:
                        sp.wait_ge(keep_cv, n)
                    sp.dma_start(mst[:], t["mask1"][b:b + 1, j * 512:(j + 1) * 512].broadcast_to([P, 512]))\
                      .then_inc(mst_in, 16)

            def features(n):
                if n >= 1:
                    sp.wait_ge(clo_done, C * n)
                b, g = n // 4, n % 4
                sp.dma_start(cT[:], t["ctxT"][b].rearrange("(c p) s -> p c s", p=P)[:, :, g * 512:(g + 1) * 512])\
                  .then_inc(ct_in, 16)

            mask(0)
            for n in range(5):
                features(n)
            for b in range(B):
                if b + 1 < B:
                    mask(b + 1)
                for g in range(QUADS):
                    u = 4 * b + g
                    if u + 5 < 4 * B:
                        features(u + 5)
                    sp.wait_ge(ao_ready, u + 1)
                    sp.dma_start(t["ao1_d"][b, :, g * P:(g + 1) * P], ao[:, u % 2, :]).then_inc(ao_out[u % 2], 16)
            for done in ao_out:
                sp.wait_ge(done, 16 * 2 * B)

        @block.gpsimd
        def _(pool):
            pool.memset(qb_hi[:], 0.0).then_inc(zero_done, 1)
            pool.memset(qb_lo[:], 0.0).then_inc(zero_done, 1)
            for par in range(2):
                pool.memset(v[:, par, :, :, DH1:DH1 + 1], 1.0).then_inc(ones_ready, 1)
            pool.wait_ge(zero_done, 2)
            pool.wait_ge(ones_ready, 2)

            def q_blocks(u):
                b, g = u // 4, u % 4
                if u >= 2:
                    pool.wait_ge(pv_mm, NT * (u - 1))
                for h in range(4):
                    r = slice(DH1 * h, DH1 * h + DH1)
                    for k, (src, dst) in enumerate(((q_hi, qb_hi), (q_lo, qb_lo))):
                        pool.tensor_copy(dst[r, u % 2, h * P:(h + 1) * P], src[r, g, b * P:(b + 1) * P])\
                            .then_inc(qb_ready, 1)
                        pool.wait_ge(qb_ready, 8 * u + 2 * h + k + 1)

            for u in range(4 * B):
                q_blocks(u)

        @block.scalar
        def _(act):
            act.wait_ge(vec_in, 48)

            def split(n, c):
                if c == 0:
                    act.wait_ge(ct_in, 16 * (n + 1))
                    if n >= 1:
                        act.wait_ge(proj_mm, PU * n)
                act.activation(c_hi[:, c, :], cT[:, c, :], ACT.Copy).then_inc(chi_done, 1)

            def project(n, i):
                b, g = n // 4, n % 4
                m = PU * n + i
                if i < 4:
                    act.wait_ge(k_ready, 4 * n + i + 1)
                    if b >= 2 and g == 0 and i == 0:
                        act.wait_ge(pv_mm, NT * 4 * (b - 1))
                    act.activation(k_hi[:, b % 2, i, g * 512:(g + 1) * 512], k32[:], ACT.Copy).then_inc(khi_done, 1)
                else:
                    act.wait_ge(proj_mm, m + 1)
                    act.activation(v[:, b % 2, 4 * g + i - 4, :, 0:DH1], heads(ps[:, bank_p(m), :], DH1),
                                   ACT.Copy).then_inc(vhi_done, 1)

            for n in range(4):
                for c in range(C):
                    split(n, c)
                for i in range(PU):
                    project(n, i)
            for c in range(C):
                split(4, c)
            for u in range(4 * B):
                b, g = u // 4, u % 4
                if u + 4 < 4 * B:
                    for i in range(PU):
                        project(u + 4, i)
                if g == 0:
                    act.wait_ge(mcol_ready, b + 1)
                for s in range(NT):
                    n = NT * u + s
                    act.wait_ge(s_mm, n + 1)
                    if n >= 2:
                        act.wait_ge(plo_done, n - 1)
                    act.activation(p32[:, s % 2, :], ps[:, s % 2, :], ACT.Exp, bias=mcol[:, s:s + 1])\
                       .then_inc(exp_done, 1)
                    act.wait_ge(exp_done, n + 1)
                    if n >= 2:
                        act.wait_ge(pv_mm, n - 1)
                    act.activation(p_hi[:, s % 2, :], p32[:, s % 2, :], ACT.Copy).then_inc(phi_done, 1)
                    if s % 3 == 2 and s // 3 < C and u + 5 < 4 * B:
                        split(u + 5, s // 3)
                act.wait_ge(pv_mm, NT * (u + 1))
                if u >= 1:
                    act.wait_ge(ao_ready, u)
                act.activation(o32[:].rearrange("p h d -> p (h d)"), ps[:, PV, 0:4 * (DH1 + 1)], ACT.Copy)\
                   .then_inc(o_evac, 1)

        @block.vector
        def _(dve):
            step = Steps(dve, dve_step)
            dve.wait_ge(vec_in, 48)
            dve.tensor_scalar(kcol[:], mcol32[:], 0.0, None, ALU.not_equal).then_inc(kcol_ready, 1)
            dve.wait_ge(kcol_ready, 1)

            def read_mask(b):
                for j in range(4):
                    n = 4 * b + j
                    dve.wait_ge(mst_in, 16 * (n + 1))
                    dve.tensor_scalar(keeprow[:, j * 512:(j + 1) * 512], mst[:], 0.0, None, ALU.not_equal)\
                       .then_inc(keep_cv, 1)
                dve.wait_ge(keep_cv, 4 * (b + 1))

            def biases(b):
                if b >= 1:
                    dve.wait_ge(exp_done, NT * 4 * b)
                step(dve.tensor_reduce(some[:], keeprow[:], AX.X, ALU.max))
                step(dve.tensor_scalar(some[:], some[:], 1e9, None, ALU.mult))
                dve.tensor_scalar(mcol[:], kcol[:, b, :], 1.0, some[:], ALU.subtract, ALU.mult).then_inc(mcol_ready, 1)
                step(dve.tensor_scalar(biasrow[:], keeprow[:], 1.0, some[:], ALU.subtract, ALU.mult))

            def split(n, c):
                dve.wait_ge(chi_done, C * n + c + 1)
                dve.tensor_tensor(c_lo[:, c, :], cT[:, c, :], c_hi[:, c, :], ALU.subtract).then_inc(clo_done, 1)

            def project(n, i):
                b, g = n // 4, n % 4
                m = PU * n + i
                if i < 4:
                    dve.wait_ge(proj_mm, m + 1)
                    if 4 * n + i >= 1:
                        dve.wait_ge(klo_done, 4 * n + i)
                    dve.scalar_tensor_tensor(k32[:], ps[:, bank_p(m), :], bk[:, i:i + 1],
                                             keeprow[:, g * 512:(g + 1) * 512], ALU.add, ALU.mult)\
                       .then_inc(k_ready, 1)
                    dve.wait_ge(khi_done, 4 * n + i + 1)
                    cols = slice(g * 512, (g + 1) * 512)
                    dve.tensor_tensor(k_lo[:, b % 2, i, cols], k32[:], k_hi[:, b % 2, i, cols], ALU.subtract)\
                       .then_inc(klo_done, 1)
                else:
                    dve.wait_ge(vhi_done, 4 * n + i - 3)
                    vp = v[:, b % 2, 4 * g + i - 4]
                    dve.tensor_tensor(vp[:, :, DH1 + 1:VW], heads(ps[:, bank_p(m), :], DH1), vp[:, :, 0:DH1],
                                      ALU.subtract).then_inc(vlo_done, 1)

            def maximum(u, k):
                n = NT * u + k
                dve.wait_ge(max_mm, n + 1)
                if n >= 1:
                    dve.wait_ge(max_done, n)
                dve.tensor_tensor_reduce(junk[:], ps[:, bank_m(n), :], biasrow[:, (k % 4) * 512:(k % 4 + 1) * 512],
                                         1.0, -3e38, ALU.add, ALU.max, mx[:, k // 4, k % 4:k % 4 + 1])\
                   .then_inc(max_done, 1)

            read_mask(0)
            for n in range(4):
                for c in range(C):
                    split(n, c)
                for i in range(PU):
                    project(n, i)
            for c in range(C):
                split(4, c)
            for u in range(4 * B):
                b, g = u // 4, u % 4
                if g == 0:
                    biases(b)
                    if b + 1 < B:
                        read_mask(b + 1)
                for i in range(PU):
                    if u + 4 < 4 * B:
                        project(u + 4, i)
                    maximum(u, 2 * i)
                    maximum(u, 2 * i + 1)
                dve.wait_ge(max_done, NT * (u + 1))
                step(dve.tensor_reduce(m4[:], mx[:], AX.X, ALU.max))
                if u >= 1:
                    dve.wait_ge(s_mm, NT * u)
                for h in range(4):
                    dve.tensor_scalar(Dg[:, h, :], identb[:], m4[:, h:h + 1], -1.0, ALU.mult, ALU.mult)\
                       .then_inc(d_ready, 1)
                for s in range(NT):
                    n = NT * u + s
                    dve.wait_ge(phi_done, n + 1)
                    if n >= 2:
                        dve.wait_ge(pv_mm, n - 1)
                    dve.tensor_tensor(p_lo[:, s % 2, :], p32[:, s % 2, :], p_hi[:, s % 2, :], ALU.subtract)\
                       .then_inc(plo_done, 1)
                    if s % 3 == 2 and s // 3 < C and u + 5 < 4 * B:
                        split(u + 5, s // 3)
                dve.wait_ge(o_evac, u + 1)
                step(dve.reciprocal(rs[:], o32[:, :, DH1]))
                if u >= 2:
                    dve.wait_ge(ao_out[u % 2], 16 * (u // 2))
                step(dve.tensor_tensor(heads(ao[:, u % 2, :], DH1), o32[:, :, 0:DH1], per_head(rs[:], 4, DH1),
                                       ALU.mult))
                dve.tensor_tensor(ao[:, u % 2, :], ao[:, u % 2, :], bv[:, g * P:(g + 1) * P], ALU.add)\
                   .then_inc(ao_ready, 1)

        @block.tensor
        def _(pe):
            def project(n, i):
                m = PU * n + i
                if i == 0:
                    pe.wait_ge(clo_done, C * (n + 1))
                if m >= 2:
                    i2, n2 = (i - 2) % PU, n if i >= 2 else n - 1
                    if i2 < 4:
                        pe.wait_ge(k_ready, 4 * n2 + i2 + 1)
                    else:
                        pe.wait_ge(vlo_done, 4 * n2 + i2 - 3)
                out = ps[:, bank_p(m), :]
                tile = slice((i % 4) * P, (i % 4 + 1) * P)
                for c in range(C):
                    if i < 4:
                        ops = ((w_hi[:, 0, c, tile], c_hi[:, c, :]), (w_hi[:, 0, c, tile], c_lo[:, c, :]),
                               (w_lo[:, 0, c, tile], c_hi[:, c, :]))
                    else:
                        ops = ((c_hi[:, c, tile], w_hi[:, 1, c, :]), (c_hi[:, c, tile], w_lo[:, 1, c, :]),
                               (c_lo[:, c, tile], w_hi[:, 1, c, :]))
                    for k, (a, m_) in enumerate(ops):
                        last = pe.matmul(out, a, m_, start=(c == 0 and k == 0), stop=(c == C - 1 and k == 2))
                last.then_inc(proj_mm, 1)

            def maximum(u, k):
                n = NT * u + k
                if k == 0:
                    pe.wait_ge(qb_ready, 8 * (u + 1))
                    pe.wait_ge(klo_done, 16 * (u // 4 + 1))
                if n >= 3:
                    pe.wait_ge(max_done, n - 2)
                h, kt = k // 4, k % 4
                pe.matmul(ps[:, bank_m(n), :], qb_hi[:, u % 2, h * P:(h + 1) * P],
                          k_hi[:, (u // 4) % 2, u % 4, kt * 512:(kt + 1) * 512], start=True, stop=True)\
                  .then_inc(max_mm, 1)

            def scores(u, s):
                n = NT * u + s
                if s == 0:
                    pe.wait_ge(d_ready, 4 * (u + 1))
                if n >= 2:
                    pe.wait_ge(exp_done, n - 1)
                out = ps[:, s % 2, :]
                par, g, tile = (u // 4) % 2, u % 4, slice(s * P, (s + 1) * P)
                pe.matmul(out, onesb[:], Dg[:].rearrange("p h q -> p (h q)"), start=True, stop=False)
                pe.matmul(out, k_hi[:, par, g, tile], qb_hi[:, u % 2, :], start=False, stop=False)
                pe.matmul(out, k_hi[:, par, g, tile], qb_lo[:, u % 2, :], start=False, stop=False)
                pe.matmul(out, k_lo[:, par, g, tile], qb_hi[:, u % 2, :], start=False, stop=True).then_inc(s_mm, 1)

            def values(u, s):
                n = NT * u + s
                if s == 0:
                    pe.wait_ge(vlo_done, 16 * (u // 4 + 1))
                    pe.wait_ge(ones_ready, 2)
                    if u >= 1:
                        pe.wait_ge(o_evac, u)
                pe.wait_ge(plo_done, n + 1)
                for h in range(4):
                    vh = v[:, (u // 4) % 2, s, 4 * (u % 4) + h]
                    o = ps[:, PV, h * (DH1 + 1):(h + 1) * (DH1 + 1)]
                    ph, pl = p_hi[:, s % 2, h * P:(h + 1) * P], p_lo[:, s % 2, h * P:(h + 1) * P]
                    pe.matmul(o, ph, vh[:, 0:DH1 + 1], start=(s == 0 and h == 0), stop=False, skip_group_check=True)
                    pe.matmul(o[:, 0:DH1], ph, vh[:, DH1 + 1:VW], start=False, stop=False, skip_group_check=True)
                    last = pe.matmul(o, pl, vh[:, 0:DH1 + 1], start=False, stop=(s == NT - 1 and h == 3),
                                     skip_group_check=True)
                last.then_inc(pv_mm, 1)

            for n in range(4):
                for i in range(PU):
                    project(n, i)
            for u in range(4 * B):
                for i in range(PU):
                    if u + 4 < 4 * B:
                        project(u + 4, i)
                    maximum(u, 2 * i)
                    maximum(u, 2 * i + 1)
                scores(u, 0)
                for s in range(1, NT):
                    scores(u, s)
                    values(u, s - 1)
                values(u, NT - 1)


def project_back(nc, t, X, src, w, bias, sb, sem, tag="b1"):
    ps, identf = t["ps"], t["identf"]
    a = sb(f"{tag}_a", [P, B, D], F32)
    aT = sb(f"{tag}_at", [P, C, TOK], F32)
    wo = sb(f"{tag}_w", [P, C, D], F32)
    bo = sb(f"{tag}_b", [P, D], F32)
    turn = Turn(sem, tag, C, [0, 1, 2, 3])
    x_in, a_in, w_in, b_in = sem(f"{tag}_x_in"), sem(f"{tag}_a_in"), sem(f"{tag}_w_in"), sem(f"{tag}_b_in")
    mm, xb, done = sem(f"{tag}_mm"), sem(f"{tag}_xb"), sem(f"{tag}_done")

    with nc.Block() as block:

        @block.sync
        def _(sp):
            sp.dma_start(a[:], src.rearrange("b p n -> p b n")).then_inc(a_in, 16)
            sp.dma_start(wo[:], w.rearrange("(c p) n -> p c n", p=P)).then_inc(w_in, 16)
            sp.dma_start(X[:], t["x_d"].rearrange("b p d -> p b d")).then_inc(x_in, 16)
            sp.dma_start(bo[:], row(bias, D)).then_inc(b_in, 16)

        @block.scalar
        def _(act):
            turn.scalar(act, ps, aT)

        @block.vector
        def _(dve):
            dve.wait_ge(x_in, 16)
            dve.wait_ge(b_in, 16)
            for b in range(B):
                dve.tensor_tensor(X[:, b, :], X[:, b, :], bo[:], ALU.add).then_inc(xb, 1)
            dve.wait_ge(xb, B)
            for b in range(B):
                dve.wait_ge(mm, b + 1)
                dve.tensor_tensor(X[:, b, :], X[:, b, :], ps[:, 4 + b, :], ALU.add).then_inc(done, 1)
            dve.wait_ge(done, B)

        @block.tensor
        def _(pe):
            pe.wait_ge(a_in, 16)
            turn.tensor(pe, ps, a, identf)
            pe.wait_ge(w_in, 16)
            pe.wait_ge(turn.copied, C)
            for b in range(B):
                for c in range(C):
                    last = pe.matmul(ps[:, 4 + b, :], aT[:, c, b * P:(b + 1) * P], wo[:, c, :],
                                     start=(c == 0), stop=(c == C - 1))
                last.then_inc(mm, 1)


def local1(nc, t, X, sb, sem):
    ps, identf = t["ps"], t["identf"]
    Hn = sb("l_h", [P, B, D], F32)
    HT = sb("l_ht", [P, C, TOK], F32)
    PT_ = sb("l_pht", [P, C, TOK], F32)
    w = sb("l_w", [P, 5, C, D], F32)
    bc = sb("l_bc", [P, 3, C], F32)
    br = sb("l_br", [P, 2, D], F32)
    prefix = sb("l_prefix", [P, P], F32)
    inv = sb("l_inv", [P, P], F32)
    lower = sb("l_lower", [P, P], F32)
    shift = sb("l_shift", [P, P], F32)
    neg = sb("l_neg", [P, P], F32)
    qkp = sb("l_qkp", [P, 3, C, TOK], F32)
    vv = sb("l_vv", [P, 2, B, D], F32)
    sc = sb("l_sc", [P, B, P], F32)
    r1 = sb("l_r1", [P, B, P], F32)
    r2 = sb("l_r2", [P, B, P], F32)
    ph = sb("l_ph", [P, B, P], F32)
    m8a = sb("l_m8a", [P, B, 8], F32)
    m8b = sb("l_m8b", [P, B, 8], F32)
    z = sb("l_z", [P, B, 8], F32)
    ex = sb("l_ex", [P, B, P], F32)
    wt = sb("l_wt", [P, 2, B, P], F32)
    wT = sb("l_wT", [P, 2, TOK], F32)
    norm = Norm(sb, sem, "ln")
    turn = Turn(sem, "lt", C, [0, 1, 2, 3])
    w_in = [sem(f"l_w_in{i}") for i in range(5)]
    c_in = sem("l_c_in")
    dve_step, act_step = sem("l_dve"), sem("l_act")
    pf_mm, pf_cp, f_mm, f_cp, v_mm, v_cp = (sem("l_pfmm"), sem("l_pfcp"), sem("l_fmm"), sem("l_fcp"), sem("l_vmm"),
                                            sem("l_vcp"))
    s_mm, m_ready, e_done, w_ready, w_turn, w_cp, o_mm, done = (
        sem("l_smm"), sem("l_mr"), sem("l_ed"), sem("l_wr"), sem("l_wturn"), sem("l_wcp"), sem("l_omm"), sem("l_done"))

    with nc.Block() as block:

        @block.sync
        def _(sp):
            for dst, src in ((prefix, "prefix"), (inv, "inv_place"), (lower, "lower"), (shift, "shift"), (bc, "l_bc"),
                             ):
                sp.dma_start(dst[:], t[src]).then_inc(c_in, 16)
            for k, name in enumerate(("L1_attn_v_b", "L1_attn_pv_b")):
                sp.dma_start(br[:, k, :], row(t[name], D)).then_inc(c_in, 16)
            for i, name in enumerate(("qT", "kT", "pkT", "vT", "pvT")):
                sp.dma_start(w[:, i], t[f"l_{name}"].rearrange("(c p) n -> p c n", p=P)).then_inc(w_in[i], 16)

        @block.scalar
        def _(act):
            norm.scalar(act)
            turn.scalar(act, ps, HT)
            act.wait_ge(c_in, 7 * 16)
            for n in range(3 * C):
                act.wait_ge(f_mm, n + 1)
                act.activation(qkp[:, n // C, n % C, :], ps[:, 4 + n % 2, :], ACT.Identity,
                               bias=bc[:, n // C, n % C:n % C + 1]).then_inc(f_cp, 1)
            act.wait_ge(m_ready, 1)
            for b in range(B):
                act.activation(ex[:, b, :], sc[:, b, :], ACT.Exp, bias=z[:, b, 2:3]).then_inc(e_done, 1)
                act.activation(z[:, b, 4:5], z[:, b, 0:1], ACT.Exp, bias=z[:, b, 2:3]).then_inc(e_done, 1)
            for k in range(2):
                act.wait_ge(w_turn, k + 1)
                act.activation(wT[:, k, :], ps[:, k, :], ACT.Copy).then_inc(w_cp, 1)

        @block.vector
        def _(dve):
            step = Steps(dve, dve_step)
            norm.vector(dve, step, Hn, X)
            dve.wait_ge(c_in, 7 * 16)
            for c in range(C):
                dve.wait_ge(pf_mm, c + 1)
                dve.tensor_tensor(PT_[:, c, :].rearrange("p (b t) -> p b t", b=B),
                                  ps[:, 6 + c % 2, :].rearrange("p (b t) -> p b t", b=B),
                                  inv[:].unsqueeze(1).to_broadcast([P, B, P]), ALU.mult).then_inc(pf_cp, 1)
            step(dve.tensor_scalar(neg[:], lower[:], 1.0, BIG, ALU.subtract, ALU.mult))
            for n in range(2 * B):
                k, b = n // B, n % B
                dve.wait_ge(v_mm, n + 1)
                dve.tensor_tensor(vv[:, k, b, :], ps[:, 6 + n % 2, :], br[:, k, :], ALU.add).then_inc(v_cp, 1)
            dve.wait_ge(s_mm, 2)
            low4 = lower[:].unsqueeze(1).to_broadcast([P, B, P])
            neg4 = neg[:].unsqueeze(1).to_broadcast([P, B, P])
            sh4 = shift[:].unsqueeze(1).to_broadcast([P, B, P])
            s4 = ps[:, 0, :].rearrange("p (b s) -> p b s", b=B)
            p4 = ps[:, 1, :].rearrange("p (b s) -> p b s", b=B)
            step(dve.scalar_tensor_tensor(sc[:], s4, D ** -0.5, low4, ALU.mult, ALU.mult))
            step(dve.tensor_tensor(sc[:], sc[:], neg4, ALU.add))
            step(dve.scalar_tensor_tensor(ph[:], p4, D ** -0.5, sh4, ALU.mult, ALU.mult))
            step(dve.tensor_reduce(z[:, :, 0], ph[:], AX.X, ALU.add))
            for b in range(B):
                last = dve.max(m8a[:, b, :], sc[:, b, :])
            step(last)
            for b in range(B):
                last = dve.match_replace(r1[:, b, :], m8a[:, b, :], sc[:, b, :], -2 * BIG)
            step(last)
            for b in range(B):
                last = dve.max(m8b[:, b, :], r1[:, b, :])
            step(last)
            for b in range(B):
                last = dve.match_replace(r2[:, b, :], m8b[:, b, :], r1[:, b, :], -2 * BIG)
            step(last)
            step(dve.tensor_tensor(z[:, :, 1], m8a[:, :, 0], z[:, :, 0], ALU.max))
            dve.tensor_scalar(z[:, :, 2], z[:, :, 1], -1.0, None, ALU.mult).then_inc(m_ready, 1)
            step(dve.tensor_tensor(r1[:], r2[:], sc[:], ALU.not_equal))
            step(dve.tensor_tensor(r1[:], r1[:], sh4, ALU.add))
            dve.wait_ge(e_done, 2 * B)
            step(dve.tensor_tensor(wt[:, 0], ex[:], r1[:], ALU.mult))
            step(dve.tensor_reduce(z[:, :, 3], wt[:, 0], AX.X, ALU.add))
            step(dve.tensor_tensor(z[:, :, 3], z[:, :, 3], z[:, :, 4], ALU.add))
            step(dve.reciprocal(z[:, :, 5], z[:, :, 3]))
            step(dve.tensor_tensor(z[:, :, 6], z[:, :, 4], z[:, :, 5], ALU.mult))
            dve.tensor_tensor(wt[:, 0], wt[:, 0], per_head(z[:, :, 5], B, P), ALU.mult).then_inc(w_ready, 1)
            dve.tensor_tensor(wt[:, 1], sh4, per_head(z[:, :, 6], B, P), ALU.mult).then_inc(w_ready, 1)
            for b in range(B):
                dve.wait_ge(o_mm, b + 1)
                dve.tensor_tensor(X[:, b, :], X[:, b, :], ps[:, 4 + b, :], ALU.add).then_inc(done, 1)
            dve.wait_ge(done, B)

        @block.tensor
        def _(pe):
            pe.wait_ge(norm.done, B)
            turn.tensor(pe, ps, Hn, identf)
            pe.wait_ge(c_in, 7 * 16)
            for c in range(C):
                if c >= 2:
                    pe.wait_ge(pf_cp, c - 1)
                for b in range(B):
                    last = pe.matmul(ps[:, 6 + c % 2, b * P:(b + 1) * P], Hn[:, b, c * P:(c + 1) * P], prefix[:],
                                     start=True, stop=True)
                last.then_inc(pf_mm, 1)
            pe.wait_ge(turn.copied, C)
            for n in range(3 * C):
                k, o = n // C, n % C
                if o == 0:
                    pe.wait_ge(w_in[k], 16)
                if n == 2 * C:
                    pe.wait_ge(pf_cp, C)
                if n >= 2:
                    pe.wait_ge(f_cp, n - 1)
                for c in range(C):
                    last = pe.matmul(ps[:, 4 + n % 2, :], w[:, k, c, o * P:(o + 1) * P],
                                     (HT if k < 2 else PT_)[:, c, :], start=(c == 0), stop=(c == C - 1))
                last.then_inc(f_mm, 1)
            for n in range(2 * B):
                k, b = n // B, n % B
                if b == 0:
                    pe.wait_ge(w_in[3 + k], 16)
                if n >= 2:
                    pe.wait_ge(v_cp, n - 1)
                for c in range(C):
                    last = pe.matmul(ps[:, 6 + n % 2, :], (HT, PT_)[k][:, c, b * P:(b + 1) * P], w[:, 3 + k, c, :],
                                     start=(c == 0), stop=(c == C - 1))
                last.then_inc(v_mm, 1)
            pe.wait_ge(f_cp, 3 * C)
            for k in range(2):
                for b in range(B):
                    tok = slice(b * P, (b + 1) * P)
                    for c in range(C):
                        last = pe.matmul(ps[:, k, tok], qkp[:, 0, c, tok], qkp[:, 1 + k, c, tok],
                                         start=(c == 0), stop=(c == C - 1))
                last.then_inc(s_mm, 1)
            for k in range(2):
                pe.wait_ge(w_ready, k + 1)
                for b in range(B):
                    last = pe.transpose(ps[:, k, b * P:(b + 1) * P], wt[:, k, b, :], identf[:])
                last.then_inc(w_turn, 1)
            pe.wait_ge(w_cp, 2)
            pe.wait_ge(v_cp, 2 * B)
            for b in range(B):
                tok = slice(b * P, (b + 1) * P)
                pe.matmul(ps[:, 4 + b, :], wT[:, 0, tok], vv[:, 0, b, :], start=True, stop=False)
                pe.matmul(ps[:, 4 + b, :], wT[:, 1, tok], vv[:, 1, b, :], start=False, stop=True).then_inc(o_mm, 1)


FF = 1408
CF = FF // P
QMAX = 127.0
ROUND = 1.5 * 2.0 ** 23
TINY = 1e-30


def ffn1(nc, t, X, out, sb, sem):
    ps, identf, identb = t["ps"], t["identf"], t["identb"]
    wst = sb("q_wst", [P, 2, CF, D], F32)
    wqt = sb("q_wqt", [P, 2, C, FF], BF16)
    wdt = sb("q_wdt", [P, CF, D], BF16)
    wi = sb("q_wi", [P, 2, FF], F32)
    wib = sb("q_wib", [P, 2, FF], BF16)
    sw = sb("q_sw", [P, 2, 2, CF], F32)
    swd = sb("q_swd", [P, 2, C], F32)
    Hn = sb("q_h", [P, B, D], F32)
    hq = sb("q_hq", [P, B, D], BF16)
    hqT = sb("q_hqt", [P, C, TOK], BF16)
    sx = sb("q_sx", [P, 8], F32)
    clip = sb("q_clip", [P, 2], F32)
    sg = sb("q_sg", [P, 2], F32)
    am = sb("q_am", [P, 2, CF], F32)
    gs = sb("q_gs", [P, 2, CF], F32)
    act_g = sb("q_actg", [P, 2, TOK], F32)
    hid = sb("q_hid", [P, CF, TOK], F32)
    hidq = sb("q_hidq", [P, CF, TOK], BF16)
    dd = sb("q_dd", [P, C, P], F32)
    srow = sb("q_srow", [P, D], F32)
    onesf = sb("q_ones", [P, P], F32)
    norm = Norm(sb, sem, "qn")
    w_in = [sem("q_w_in0"), sem("q_w_in1"), sem("q_w_in2")]
    gs_ready = sem("q_gsr")
    clip_in, out_sem = sem("q_clip_in"), sem("q_out")
    dve_step = sem("q_dve")
    sg_done, wq_ready, w_turn, w_cp = sem("q_sgd"), sem("q_wqr"), sem("q_wt"), sem("q_wcp")
    am_ready, am_all = sem("q_amr"), sem("q_ama")
    hq_ready, h_turn, h_cp = sem("q_hqr"), sem("q_ht"), sem("q_hc")
    g_mm, g_act, h_mul, hq2, o_mm, done, d_ready, d_mm = (
        sem("q_gmm"), sem("q_gact"), sem("q_hmul"), sem("q_hq2"), sem("q_omm"), sem("q_done"), sem("q_dr"), sem("q_dmm"))
    NW = 2 * CF + C

    def psb(n):
        return ps[:, 2 * (n % 2):2 * (n % 2) + 2, :].rearrange("p a b -> p (a b)").bitcast(BF16)\
            .rearrange("p (c n) -> p c n", n=P)

    def psh():
        return ps[:, 4:6, :].rearrange("p a b -> p (a b)").bitcast(BF16)

    with nc.Block() as block:

        @block.sync
        def _(sp):
            sp.dma_start(clip[:], t["clips"].rearrange("(a n) -> a n", a=1).broadcast_to([P, 2])).then_inc(clip_in, 16)
            for k, name in enumerate(("w_gate", "w_up")):
                sp.dma_start(wst[:, k], t[f"L1_ffn_{name}"].rearrange("(c p) n -> p c n", p=P)).then_inc(w_in[k], 16)
            sp.wait_ge(wq_ready, CF)
            sp.dma_start(wst[:, 0].rearrange("p c n -> p (c n)").rearrange("p (c n) -> p c n", n=FF),
                         t["L1_ffn_w_down"].rearrange("(c p) n -> p c n", p=P)).then_inc(w_in[2], 16)
            for b in range(B):
                sp.wait_ge(done, b + 1)
                sp.dma_start(out[b], X[:, b, :]).then_inc(out_sem, 16)
            sp.wait_ge(out_sem, 16 * B)

        @block.gpsimd
        def _(pool):
            pool.memset(onesf[:], 1.0).then_inc(d_ready, 1)
            for k in range(2):
                pool.wait_ge(am_ready, k + 1)
                pool.partition_all_reduce(sx[:, 2 + k:3 + k], sx[:, k:k + 1], P, bass.bass_isa.ReduceOp.max)\
                    .then_inc(am_all, 1)
                pool.wait_ge(am_all, k + 1)

        @block.scalar
        def _(act):
            act.wait_ge(clip_in, 16)
            act.activation(sg[:], clip[:], ACT.Sigmoid).then_inc(sg_done, 1)

            def turned(n):
                act.wait_ge(w_turn, n + 1)
                if n < 2 * CF:
                    act.activation(wqt[:, n // CF, :, (n % CF) * P:(n % CF + 1) * P],
                                   psb(n)[:, 0:C, :], ACT.Copy).then_inc(w_cp, 1)
                else:
                    act.activation(wdt[:, :, (n - 2 * CF) * P:(n - 2 * CF + 1) * P], psb(n)[:, 0:CF, :], ACT.Copy)\
                       .then_inc(w_cp, 1)

            for n in range(NW):
                turned(n)
            norm.scalar(act)
            act.wait_ge(h_turn, 1)
            act.activation(hqT[:].rearrange("p c t -> p (c t)"), psh(), ACT.Copy).then_inc(h_cp, 1)
            act.wait_ge(gs_ready, 1)
            for i in range(CF):
                act.wait_ge(g_mm, 2 * i + 2)
                if i >= 2:
                    act.wait_ge(h_mul, i - 1)
                act.activation(act_g[:, i % 2, :], ps[:, 4 + (2 * i) % 4, :], ACT.Silu, scale=gs[:, 0, i:i + 1])\
                   .then_inc(g_act, 1)

        @block.vector
        def _(dve):
            step = Steps(dve, dve_step)
            for n in range(NW):
                k, i = (n // CF, n % CF) if n < 2 * CF else (2, n - 2 * CF)
                src = wst[:, k, i, :] if k < 2 else \
                    wst[:, 0].rearrange("p c n -> p (c n)").rearrange("p (c n) -> p c n", n=FF)[:, i, :]
                w = D if k < 2 else FF
                if i == 0:
                    dve.wait_ge(w_in[k], 16)
                sc, rc = (sw[:, k, 0, i:i + 1], sw[:, k, 1, i:i + 1]) if k < 2 else \
                    (swd[:, 0, i:i + 1], swd[:, 1, i:i + 1])
                step(dve.tensor_reduce(am[:, 0, 0:1], src, AX.X, ALU.max, apply_absolute_value=True))
                step(dve.tensor_scalar(sc, am[:, 0, 0:1], 1.0 / QMAX, TINY, ALU.mult, ALU.max))
                step(dve.reciprocal(rc, sc))
                step(dve.tensor_scalar(wi[:, 0, 0:w], src, rc, ROUND, ALU.mult, ALU.add))
                if n >= 2:
                    dve.wait_ge(w_turn, n - 1)
                dve.tensor_scalar(wib[:, n % 2, 0:w], wi[:, 0, 0:w], ROUND, None, ALU.subtract).then_inc(wq_ready, 1)
                dve.wait_ge(wq_ready, n + 1)
            norm.vector(dve, step, Hn, X)
            dve.wait_ge(norm.done, B)
            dve.tensor_reduce(sx[:, 0:1], Hn[:].rearrange("p b d -> p (b d)"), AX.X, ALU.max,
                              apply_absolute_value=True).then_inc(am_ready, 1)
            dve.wait_ge(am_all, 1)
            dve.wait_ge(sg_done, 1)

            def quantise(k, dst, src, w):
                step(dve.tensor_tensor(sx[:, 4 + k:5 + k], sx[:, 2 + k:3 + k], sg[:, k:k + 1], ALU.mult))
                step(dve.tensor_scalar(sx[:, 4 + k:5 + k], sx[:, 4 + k:5 + k], 1.0 / QMAX, TINY, ALU.mult, ALU.max))
                step(dve.reciprocal(sx[:, 6 + k:7 + k], sx[:, 4 + k:5 + k]))
                for i in range(len(src)):
                    step(dve.tensor_scalar(wi[:, 0, 0:w], src[i], sx[:, 6 + k:7 + k], ROUND, ALU.mult, ALU.add))
                    step(dve.tensor_scalar(wi[:, 1, 0:w], wi[:, 0, 0:w], ROUND, QMAX, ALU.subtract, ALU.min))
                    dve.tensor_scalar(dst[i], wi[:, 1, 0:w], -QMAX - 1.0, None, ALU.max)\
                       .then_inc(hq_ready if k == 0 else hq2, 1)

            quantise(0, [hq[:, b, :] for b in range(B)], [Hn[:, b, :] for b in range(B)], D)
            dve.tensor_scalar(gs[:], sw[:, :, 0, :], sx[:, 4:5], None, ALU.mult).then_inc(gs_ready, 1)
            dve.wait_ge(gs_ready, 1)
            for i in range(CF):
                dve.wait_ge(g_act, i + 1)
                dve.scalar_tensor_tensor(hid[:, i, :], ps[:, 4 + (2 * i + 1) % 4, :], gs[:, 1, i:i + 1],
                                         act_g[:, i % 2, :], ALU.mult, ALU.mult).then_inc(h_mul, 1)
            dve.wait_ge(h_mul, CF)
            step(dve.tensor_reduce(am[:, 1, :], hid[:], AX.X, ALU.max, apply_absolute_value=True))
            dve.tensor_reduce(sx[:, 1:2], am[:, 1, :], AX.X, ALU.max).then_inc(am_ready, 1)
            dve.wait_ge(am_all, 2)
            quantise(1, [hidq[:, i, :] for i in range(CF)], [hid[:, i, :] for i in range(CF)], TOK)
            step(dve.tensor_scalar(swd[:, 0, :], swd[:, 0, :], sx[:, 5:6], None, ALU.mult))
            for c in range(C):
                dve.tensor_scalar(dd[:, c, :], identf[:], swd[:, 0, c:c + 1], None, ALU.mult).then_inc(d_ready, 1)
            dve.wait_ge(d_mm, 1)
            step(dve.tensor_copy(srow[:], ps[:, 0, :]))
            for b in range(B):
                dve.wait_ge(o_mm, b + 1)
                step(dve.tensor_tensor(act_g[:, b % 2, :], ps[:, 4 + b, :], srow[:], ALU.mult))
                dve.tensor_tensor(X[:, b, :], X[:, b, :], act_g[:, b % 2, :], ALU.add).then_inc(done, 1)
            dve.wait_ge(done, B)

        @block.tensor
        def _(pe):
            for n in range(NW):
                nch = C if n < 2 * CF else CF
                pe.wait_ge(wq_ready, n + 1)
                if n >= 2:
                    pe.wait_ge(w_cp, n - 1)
                for c in range(nch):
                    last = pe.transpose(psb(n)[:, c, :], wib[:, n % 2, c * P:(c + 1) * P], identb[:])
                last.then_inc(w_turn, 1)
            pe.wait_ge(hq_ready, B)
            for c in range(C):
                for b in range(B):
                    o = c * TOK + b * P
                    last = pe.transpose(psh()[:, o:o + P], hq[:, b, c * P:(c + 1) * P], identb[:])
            last.then_inc(h_turn, 1)
            pe.wait_ge(h_cp, 1)
            pe.wait_ge(w_cp, NW)
            for i in range(CF):
                for k in range(2):
                    n = 2 * i + k
                    if n >= 4:
                        pe.wait_ge(h_mul, i - 1)
                    for c in range(C):
                        last = pe.matmul(ps[:, 4 + n % 4, :], wqt[:, k, c, i * P:(i + 1) * P], hqT[:, c, :],
                                         start=(c == 0), stop=(c == C - 1))
                    last.then_inc(g_mm, 1)
            pe.wait_ge(d_ready, 1 + C)
            for c in range(C):
                last = pe.matmul(ps[:, 0, c * P:(c + 1) * P], onesf[:], dd[:, c, :], start=True, stop=True)
            last.then_inc(d_mm, 1)
            pe.wait_ge(hq2, CF)
            for b in range(B):
                for i in range(CF):
                    last = pe.matmul(ps[:, 4 + b, :], hidq[:, i, b * P:(b + 1) * P], wdt[:, i, :],
                                     start=(i == 0), stop=(i == CF - 1))
                last.then_inc(o_mm, 1)




def build(nc, t, out):
    with ExitStack() as ctx:
        def sb(name, shape, dt):
            return ctx.enter_context(nc.sbuf_tensor(name, shape, dt))

        def sem(name):
            return ctx.enter_context(nc.semaphore(name))

        def stage(run, *args):
            sems = []

            def own_sem(name):
                sems.append(nc.alloc_semaphore(name=name))
                return sems[-1]

            with ExitStack() as own:
                run(nc, t, *args, lambda name, shape, dt: own.enter_context(nc.sbuf_tensor(name, shape, dt)), own_sem)
            nc.clear_and_free_semaphores(sems)
            nc.all_engine_barrier()

        t["ps"] = ctx.enter_context(nc.psum_tensor("ps", [P, 8, 512], F32))
        t["identf"] = sb("identf", [P, P], F32)
        t["identb"] = sb("identb", [P, P], BF16)
        t["onesb"] = sb("onesb", [P, P], BF16)
        t["lt_hi_d"] = nc.dram_tensor("lt_hi_d", (B, P, C, P), BF16, kind="Internal").ap()
        t["lt_lo_d"] = nc.dram_tensor("lt_lo_d", (B, P, C, P), BF16, kind="Internal").ap()
        t["ao_d"] = nc.dram_tensor("ao_d", (B, P, INNER), F32, kind="Internal").ap()
        t["ao1_d"] = nc.dram_tensor("ao1_d", (B, P, D), F32, kind="Internal").ap()
        t["x_d"] = nc.dram_tensor("x_d", (B, P, D), F32, kind="Internal").ap()
        eye_in, consts = sem("eye_in"), sem("consts")
        with nc.Block() as block:

            @block.sync
            def _(sp):
                sp.dma_start(t["identf"][:], t["eye"]).then_inc(eye_in, 16)

            @block.vector
            def _(dve):
                dve.memset(t["onesb"][:], 1.0).then_inc(consts, 1)
                dve.wait_ge(eye_in, 16)
                dve.tensor_copy(t["identb"][:], t["identf"][:]).then_inc(consts, 1)
                dve.wait_ge(consts, 2)

        with ExitStack() as held:
            def kept(name, shape):
                return held.enter_context(nc.sbuf_tensor(name, shape, BF16))

            keep = {"w_hi": kept("w0_hi", [P, C, QUADS, 512]), "w_lo": kept("w0_lo", [P, C, QUADS, 512]),
                    "q_hi": kept("q0_hi", [P, PAIRS, TOK]), "q_lo": kept("q0_lo", [P, PAIRS, TOK])}
            stage(cross0_prepare, keep)
            stage(cross0_attend, keep)

        with ExitStack() as held:
            def kept(name, shape):
                return held.enter_context(nc.sbuf_tensor(name, shape, BF16))

            keep = {"w_hi": kept("w1_hi", [P, 2, C, D]), "w_lo": kept("w1_lo", [P, 2, C, D]),
                    "q_hi": kept("q1_hi", [P, QUADS, TOK]), "q_lo": kept("q1_lo", [P, QUADS, TOK])}
            with ExitStack() as early:
                X = early.enter_context(nc.sbuf_tensor("xa", [P, B, D], F32))
                stage(cross0_finish, X)
                stage(self0, X)
                stage(experts, X)
                stage(cross1_prepare, X, keep)
            stage(cross1_attend, keep)

        X = sb("xb", [P, B, D], F32)
        stage(project_back, X, t["ao1_d"], t["woT1"], t["L1_xattn_bo"])
        stage(local1, X)
        stage(ffn1, X, out)


def constants():
    place = np.arange(P)
    half = RD // 2
    inv_freq = (1.0 / 10000.0 ** (np.arange(0, RD, 2, dtype=np.float32) / RD)).astype(np.float32)
    freqs = place.astype(np.float32)[:, None] * inv_freq[None, :]
    emb = np.concatenate([freqs, freqs], axis=-1)
    sin = np.sin(emb)
    sin[:, :half] = -sin[:, :half]
    same = place[:, None] // 32 == place[None, :] // 32
    return {
        "eye": np.eye(P, dtype=np.float32),
        "rope": np.stack([np.cos(emb), sin], axis=1).astype(np.float32),
        "prefix": (same & (place[:, None] <= place[None, :])).astype(np.float32),
        "inv_place": np.broadcast_to(1.0 / (place % 32 + 1.0), (P, P)).astype(np.float32),
        "lower": (place[None, :] < place[:, None]).astype(np.float32),
        "shift": (place[None, :] == place[:, None] - 1).astype(np.float32),
    }


def columns(v):
    return np.asarray(v).reshape(-1, P).T


def kernel(**inputs):
    import concourse.bacc as _bacc
    from concourse.bass_utils import run_bass_kernel_spmd as _run

    a = {name: np.asarray(v) for name, v in inputs.items()}
    mask0 = a["mask_BxS2_bf1"].view(np.uint8)
    mask1 = a["mask_Bx1xS2_ik0"].reshape(B, S2)
    arrays = {
        **constants(),
        "x": a["x"],
        "ctx": a["ctx_1024"],
        "ctxT": a["ctx_1024"].transpose(0, 2, 1),
        "mask0": mask0,
        "mask0_col": mask0.reshape(B, NT, P).transpose(2, 0, 1),
        "mask1": mask1,
        "mask1_col": mask1.reshape(B, NT, P).transpose(2, 0, 1),
        "moe_b1_col": a["L0_ffn_b1"].reshape(E, CH, P).transpose(2, 0, 1),
        "l_bc": np.stack([columns(a[f"L1_attn_{n}_b"]) for n in ("q", "k", "pk")], axis=1),
        "clips": np.concatenate([a["L1_ffn_clip_x"], a["L1_ffn_clip_down"]]),
    }
    for name in ("L0_xattn_qn_g", "L0_xattn_kn_g", "L0_xattn_Wq", "L0_xattn_Wkv", "L0_xattn_Wout", "L0_xattn_bout",
                 "L0_attn_Wq", "L0_attn_Wk", "L0_attn_Wv", "L0_attn_Wo", "L0_ffn_Wr", "L0_ffn_br", "L0_ffn_W1",
                 "L0_ffn_W2", "L0_ffn_b2", "L1_xattn_bv", "L1_xattn_bo", "L1_attn_v_b", "L1_attn_pv_b",
                 "L1_ffn_w_gate", "L1_ffn_w_up", "L1_ffn_w_down"):
        arrays[name] = a[name]
    for name in ("L0_xattn_ln_x_g", "L0_xattn_ln_x_b", "L0_xattn_ln_l_g", "L0_xattn_ln_l_b", "L1_xattn_bq",
                 "L1_xattn_bk"):
        arrays[f"{name}_col"] = columns(a[name])
    for short, name in (("wqT1", "L1_xattn_Wq"), ("wkT1", "L1_xattn_Wk"), ("wvT1", "L1_xattn_Wv"),
                        ("woT1", "L1_xattn_Wo"), ("l_qT", "L1_attn_q_w"), ("l_kT", "L1_attn_k_w"),
                        ("l_pkT", "L1_attn_pk_w"), ("l_vT", "L1_attn_v_w"), ("l_pvT", "L1_attn_pv_w")):
        arrays[short] = a[name].T
    arrays = {f"in_{name}": np.ascontiguousarray(v) for name, v in arrays.items()}
    nc = _bacc.Bacc("TRN2", target_bir_lowering=False, num_devices=1)
    t = {name[3:]: nc.dram_tensor(name, v.shape, mybir.dt.from_np(v.dtype), kind="ExternalInput").ap()
         for name, v in arrays.items()}
    out = nc.dram_tensor("out", (B, P, D), F32, kind="ExternalOutput").ap()
    build(nc, t, out)
    return _run(nc, [arrays], core_ids=[0]).results[0]["out"]
```
